# Optimizing a Trainium2 kernel written in Bass

```python
import numpy as np
import jax
import jax.numpy as jnp

def _softmax(x, axis=-1):
    return jax.nn.softmax(x, axis=axis)

def _gelu(x):
    return jax.nn.gelu(x, approximate=True)

def _silu(x):
    return jax.nn.silu(x)

def _sigmoid(x):
    return jax.nn.sigmoid(x)

def _layernorm(x, axis=-1, eps=1e-05):
    m = jnp.mean(x, axis=axis, keepdims=True)
    v = jnp.var(x, axis=axis, keepdims=True)
    return (x - m) / jnp.sqrt(v + eps)

def _scatter_add(tgt, idx, src, axis=0):
    return tgt.at[idx].add(src)

def _segment_sum(src, seg, n):
    return jax.ops.segment_sum(src, seg, n)
kernel_name = 'mk_prb_d1_jaxref_r4_306c30'

def setup_inputs(seed: int=0):
    np.random.seed(seed)
    _w = jnp.asarray

    def _L0_attn_setup():
        import jax, jax.numpy as jnp
        import numpy as np
        import math
        NH, NKV, D = (32, 8, 128)

        def _alibi_slopes(n):
            cp2 = 2 ** math.floor(math.log2(n))
            base = 2.0 ** (-8.0 / cp2)
            slopes = base ** np.arange(1, cp2 + 1, dtype=np.float32)
            if cp2 != n:
                extra_base = 2.0 ** (-4.0 / cp2)
                extra = extra_base ** np.arange(1, 1 + 2 * (n - cp2), 2, dtype=np.float32)
                slopes = np.concatenate([slopes, extra])
            return slopes.astype(np.float32)
        key = jax.random.key(seed)
        k1, k2, k3 = jax.random.split(key, 3)
        B, S, H = (4, 256, 1024)
        qkv_out = NH * D + 2 * NKV * D
        return {'hidden_states': jax.random.normal(k1, (B, S, H), jnp.float32) * 0.02, 'w_qkv': jax.random.normal(k2, (H, qkv_out), jnp.float32) * 0.02, 'w_o': jax.random.normal(k3, (NH * D, H), jnp.float32) * 0.02}
    _L0_attn_in = _L0_attn_setup()

    def _L0_ffn_setup():
        import jax, jax.numpy as jnp
        import numpy as np
        RANKS = (8, 16, 32, 64)
        TOPK = 1
        SCALING = 1.0 / 4
        key = jax.random.key(seed)
        ks = jax.random.split(key, 7)
        D_IN, D_OUT, MAX_R, N_RANKS = (1024, 1024, 64, len(RANKS))
        B_, S_ = (4, 512)
        return {'hidden_states': jax.random.normal(ks[0], (B_, S_, D_IN), jnp.float32), 'W': jax.random.normal(ks[1], (D_OUT, D_IN), jnp.float32) * 0.02, 'b': jax.random.normal(ks[2], (D_OUT,), jnp.float32) * 0.02, 'A': jax.random.normal(ks[3], (MAX_R, D_IN), jnp.float32) * 0.02, 'B': jnp.zeros((D_OUT, MAX_R), jnp.float32) + jax.random.normal(ks[4], (D_OUT, MAX_R), jnp.float32) * 0.02, 'gate_w': jax.random.normal(ks[5], (N_RANKS, D_IN), jnp.float32) * 0.02, 'gate_b': jax.random.normal(ks[6], (N_RANKS,), jnp.float32) * 0.02}
    _L0_ffn_in = _L0_ffn_setup()
    _d = {'L0_attn_hidden_states': _L0_attn_in['hidden_states'], 'L0_attn_w_qkv': _L0_attn_in['w_qkv'], 'L0_attn_w_o': _L0_attn_in['w_o'], 'L0_ffn_W': _L0_ffn_in['W'], 'L0_ffn_b': _L0_ffn_in['b'], 'L0_ffn_A': _L0_ffn_in['A'], 'L0_ffn_B': _L0_ffn_in['B'], 'L0_ffn_gate_w': _L0_ffn_in['gate_w'], 'L0_ffn_gate_b': _L0_ffn_in['gate_b']}
    _x0 = _d['L0_attn_hidden_states']
    _d['L0_attn_hidden_states'] = jax.random.normal(jax.random.fold_in(jax.random.key(seed), 1), (4, 512, 1024), dtype=_x0.dtype)
    del _x0
    return _d

def reference(L0_attn_hidden_states, L0_attn_w_qkv, L0_attn_w_o, L0_ffn_W, L0_ffn_b, L0_ffn_A, L0_ffn_B, L0_ffn_gate_w, L0_ffn_gate_b):

    def _L0_attn_ref(hidden_states, w_qkv, w_o):
        import jax, jax.numpy as jnp
        import numpy as np
        import math
        NH, NKV, D = (32, 8, 128)

        def _alibi_slopes(n):
            cp2 = 2 ** math.floor(math.log2(n))
            base = 2.0 ** (-8.0 / cp2)
            slopes = base ** np.arange(1, cp2 + 1, dtype=np.float32)
            if cp2 != n:
                extra_base = 2.0 ** (-4.0 / cp2)
                extra = extra_base ** np.arange(1, 1 + 2 * (n - cp2), 2, dtype=np.float32)
                slopes = np.concatenate([slopes, extra])
            return slopes.astype(np.float32)
        B, S, H = hidden_states.shape
        G = NH // NKV
        scale = D ** (-0.5)
        qkv = hidden_states @ w_qkv
        q = qkv[..., :NH * D].reshape(B, S, NKV, G, D)
        k = qkv[..., NH * D:NH * D + NKV * D].reshape(B, S, NKV, D)
        v = qkv[..., NH * D + NKV * D:].reshape(B, S, NKV, D)
        scores = jnp.einsum('bqhgd,bkhd->bhgqk', q, k) * scale
        slopes = jnp.asarray(_alibi_slopes(NH)).reshape(NKV, G)
        pos = jnp.arange(S)
        rel = pos[:, None] - pos[None, :]
        sqrt_dist = jnp.sqrt(jnp.maximum(rel, 0).astype(jnp.float32))
        bias = -slopes[:, :, None, None] * sqrt_dist
        bias = jnp.where(rel[None, None] >= 0, bias, -jnp.inf)
        attn = jax.nn.softmax(scores + bias[None], axis=-1)
        out = jnp.einsum('bhgqk,bkhd->bqhgd', attn, v).reshape(B, S, NH * D)
        return out @ w_o

    def _L0_ffn_ref(hidden_states, W, b, A, B, gate_w, gate_b):
        import jax, jax.numpy as jnp
        import numpy as np
        RANKS = (8, 16, 32, 64)
        TOPK = 1
        SCALING = 1.0 / 4
        bsz, seq, d_in = hidden_states.shape
        out = jnp.einsum('bsd,od->bso', hidden_states, W) + b
        x = hidden_states.reshape(-1, d_in)
        scores = x @ gate_w.T + gate_b
        probs = jax.nn.softmax(scores, axis=-1)
        routing_weights, selected = jax.lax.top_k(probs, TOPK)
        routing_weights = routing_weights / jnp.sum(routing_weights, axis=-1, keepdims=True)
        lora_outputs = jnp.stack([x @ A[:r, :].T @ B[:, :r].T for r in RANKS], axis=1)
        sel = jnp.take_along_axis(lora_outputs, selected[:, :, None], axis=1)
        final = jnp.sum(sel * routing_weights[:, :, None], axis=1)
        return out + final.reshape(bsz, seq, -1)
    x = L0_attn_hidden_states
    xn = _layernorm(x, axis=-1)
    x = x + _L0_attn_ref(xn, L0_attn_w_qkv, L0_attn_w_o) + _L0_ffn_ref(xn, L0_ffn_W, L0_ffn_b, L0_ffn_A, L0_ffn_B, L0_ffn_gate_w, L0_ffn_gate_b)
    return x

_drawn_inputs = setup_inputs


def setup_inputs(seed=0):
    import zlib

    import numpy as np

    out = dict(_drawn_inputs(seed))
    spreads = {}
    factors = {'L0_ffn_b': 3.562, 'L0_ffn_gate_b': 25.518}
    for name, (base, spread) in spreads.items():
        noise = np.random.default_rng([zlib.crc32(name.encode()), seed]).standard_normal(out[name].shape)
        drawn = base * np.exp(spread * noise) if base else spread * noise
        out[name] = jnp.asarray(drawn.astype(out[name].dtype))
    for name, factor in factors.items():
        out[name] = (out[name] * factor).astype(out[name].dtype)
    return out
```

```python
from contextlib import ExitStack

import numpy as np

import concourse.bass as bass
from concourse import mybir

ALU = mybir.AluOpType
ACT = mybir.ActivationFunctionType
AX = mybir.AxisListType
F32 = mybir.dt.float32
F32R = mybir.dt.float32r

P = 128
HIDDEN = 1024
HEADS = 32
KV_HEADS = 8
G = HEADS // KV_HEADS
D = 128
BATCH = 4
SEQ = 512
TOKENS = BATCH * SEQ
SCALE = float(D) ** -0.5
EPS = 1e-5
RANKS = (8, 16, 32, 64)
R = max(RANKS)
E = len(RANKS)

PAIRS = BATCH // 2
PT = TOKENS // PAIRS
TT = PT // P
HT = HIDDEN // P
QT = SEQ // P
UNITS = 2 * G
NP = QT * (QT + 1) // 2 * P
HALVES = HIDDEN // 512
BTILES = TT * HALVES
MASKED = 1e36
AG = R + E
LK = R + 1

OFF = [P * (i * (i + 1) // 2) for i in range(QT)]
TOFF = {0: 0, 1: 512, 3: 896, 2: 1024}

W_AG, W_T0, W_T1, W_LORA, W_T3, W_T2, W_T4, W_T5, W_T6, W_T7, W_K0, W_V0, W_Q0, W_K1 = range(14)
BEFORE = 14
C_Q1, C_O0, C_Q2, C_O1, C_Q3, C_V, C_O2, C_Q0, C_O3, C_K = range(10)
PER_GROUP = 10
L_Q1, L_O0, L_Q2, L_O1, L_Q3, L_O2, L_O3 = range(7)
CHUNKS = BEFORE + PER_GROUP * (KV_HEADS - 1) + 7

FFN_BURSTS = HT // 2
BURSTS = FFN_BURSTS + 2 * KV_HEADS
LINKS = 7 * (TT // 2) + 10


def block_program(nc, x, w_qkv, w_o, w_ffn, w_ag, w_lora, gate_b, consts, out):
    with ExitStack() as ctx:
        def sb(name, shape, dt=F32):
            return ctx.enter_context(nc.sbuf_tensor(name, shape, dt))

        def bank(name):
            return ctx.enter_context(nc.psum_tensor(name, [P, 512], F32))

        def sem(name):
            return ctx.enter_context(nc.semaphore(name))

        x_hi = sb("x_hi", [P, HT, PT], F32R)
        x_lo = sb("x_lo", [P, HT, PT], F32R)
        acc = sb("acc", [P, TT, HIDDEN])
        at_hi = sb("at_hi", [P, 2, PT], F32R)
        at_lo = sb("at_lo", [P, 2, PT], F32R)
        wo_hi = sb("wo_hi", [P, 2, HIDDEN], F32R)
        wo_lo = sb("wo_lo", [P, 2, HIDDEN], F32R)
        wq_hi = sb("wq_hi", [P, 2, HIDDEN], F32R)
        wq_lo = sb("wq_lo", [P, 2, HIDDEN], F32R)
        wkv_hi = sb("wkv_hi", [P, HIDDEN], F32R)
        wkv_lo = sb("wkv_lo", [P, HIDDEN], F32R)
        q_hi = sb("q_hi", [P, SEQ], F32R)
        q_lo = sb("q_lo", [P, SEQ], F32R)
        k_hi = sb("k_hi", [P, PT], F32R)
        k_lo = sb("k_lo", [P, PT], F32R)
        v_hi = sb("v_hi", [P, PT], F32R)
        v_lo = sb("v_lo", [P, PT], F32R)
        next_k = sb("next_k", [P, PT])
        next_v = sb("next_v", [P, PT])
        stage = sb("stage", [P, 2, HIDDEN])
        probs = sb("probs", [P, NP])
        pt_hi = sb("pt_hi", [P, NP], F32R)
        pt_lo = sb("pt_lo", [P, NP], F32R)
        dist = sb("dist", [P, SEQ])
        head_bias = sb("head_bias", [P, SEQ])
        ident = sb("ident", [P, P])
        slopes = sb("slopes", [P, HEADS])
        gbias = sb("gbias", [P, E])
        neg_max = sb("neg_max", [P, QT])
        row_sum = sb("row_sum", [P, QT])
        row_inv = sb("row_inv", [P, QT])

        ps_a, ps_b, ps_c = bank("ps_a"), bank("ps_b"), bank("ps_c")
        ps_t0, ps_t1 = bank("ps_t0"), bank("ps_t1")
        ps_o = bank("ps_o")
        ps_q, ps_kv = bank("ps_q"), bank("ps_kv")

        ag_out = next_k[:, 0:TT * AG].rearrange("p (t a) -> p t a", a=AG)
        small = next_k[:, TT * AG:TT * AG + 48]
        stats = small[:, 0:24].rearrange("p (t h s) -> p t h s", t=2, h=2)
        moments = small[:, 24:32].rearrange("p (g t m) -> p g t m", g=2, t=2)
        rstd, root, newton = small[:, 32:40], small[:, 40:42], small[:, 42:44]
        u_mask = probs[:, 0:TT * R].rearrange("p (t a) -> p t a", a=R)
        gate_buf = probs[:, TT * R:TT * (R + 2 * E)].rearrange("p (k t e) -> p k t e", k=2, e=E)
        gate_col = probs[:, TT * (R + 2 * E):TT * (R + 2 * E + 10)].rearrange("p (k t) -> p k t", t=TT)
        normed = [probs[:, 0:HIDDEN], next_v[:, :]]
        score_bank = {3: ps_c[:, :], 2: ps_b[:, 0:3 * P], 0: ps_a[:, 0:P], 1: ps_a[:, P:3 * P]}
        t_banks = [(ps_t0, 0, 512), (ps_t1, 512, 512), (ps_o, 1024, 256)]

        s_const = sem("s_const")
        s_x = [sem(f"s_x{i}") for i in range(TT // 2)]
        s_loaded = [sem("s_loaded0"), sem("s_loaded1")]
        s_w_hi = sem("s_w_hi")
        s_w_lo = sem("s_w_lo")
        s_link = sem("s_link")
        s_var = sem("s_var")
        s_std = sem("s_std")
        s_xn = sem("s_xn")
        s_xt = sem("s_xt")
        s_x_hi = sem("s_x_hi")
        s_x_lo = sem("s_x_lo")
        s_ag = sem("s_ag")
        s_ag_out = sem("s_ag_out")
        s_gate = sem("s_gate")
        s_gate_exp = sem("s_gate_exp")
        s_u = sem("s_u")
        s_ut = sem("s_ut")
        s_u_hi = sem("s_u_hi")
        s_u_lo = sem("s_u_lo")
        s_acc = sem("s_acc")
        s_burst = sem("s_burst")
        s_kv = sem("s_kv")
        s_kv_out = sem("s_kv_out")
        s_k_hi = sem("s_k_hi")
        s_k_lo = sem("s_k_lo")
        s_vt = sem("s_vt")
        s_v_hi = sem("s_v_hi")
        s_v_lo = sem("s_v_lo")
        s_q = sem("s_q")
        s_q_hi = sem("s_q_hi")
        s_q_lo = sem("s_q_lo")
        s_bias = sem("s_bias")
        s_scores = sem("s_scores")
        s_neg_max = sem("s_neg_max")
        s_exp = sem("s_exp")
        s_inv = sem("s_inv")
        s_probs = sem("s_probs")
        s_pt = sem("s_pt")
        s_pt_hi = sem("s_pt_hi")
        s_pt_lo = sem("s_pt_lo")
        s_o = sem("s_o")
        s_at_hi = sem("s_at_hi")
        s_at_lo = sem("s_at_lo")
        s_out = sem("s_out")
        s_settled = sem("s_settled")

        def unit(pr, g, n):
            return pr * (KV_HEADS * UNITS) + g * UNITS + n

        def group(pr, g):
            return pr * KV_HEADS + g

        def chunk(pr, k, g=0):
            return pr * CHUNKS + g * PER_GROUP + k

        def group_chunk(k, last):
            if not last:
                return BEFORE + k
            return BEFORE + {C_Q1: L_Q1, C_O0: L_O0, C_Q2: L_Q2, C_O1: L_O1, C_Q3: L_Q3,
                             C_O2: L_O2, C_O3: L_O3}[k]

        def burst_base(pr, b, g=0):
            return pr * (BURSTS * BTILES) + g * (2 * BTILES) + b * BTILES

        def wq(i):
            return wq_hi[:, i, :], wq_lo[:, i, :]

        def wo(i):
            return wo_hi[:, i, :], wo_lo[:, i, :]

        wkv = (wkv_hi[:, :], wkv_lo[:, :])

        block = ctx.enter_context(nc.Block())

        def settled(eng):
            eng.sem_inc(s_settled, 1)

        @block.sync
        def _(sp):
            sp.sem_inc(s_out, 16)
            sp.dma_start(dist[:, :], consts[:, 0:SEQ]).then_inc(s_const, 16)
            sp.dma_start(ident[:, :], consts[:, SEQ:SEQ + P]).then_inc(s_const, 16)
            sp.dma_start(slopes[:, :], consts[:, SEQ + P:SEQ + P + HEADS]).then_inc(s_const, 16)
            sp.dma_start(gbias[:, :], gate_b.partition_broadcast(P)).then_inc(s_const, 16)

            def load(pr, k, source, g=0, rows=P, cols=HIDDEN):
                sp.wait_ge(s_w_lo, chunk(pr, max(k - 1, 0), g) + 1)
                sp.dma_start(stage[0:rows, k % 2, 0:cols], source).then_inc(s_loaded[k % 2], 16)

            def qkv(c):
                return w_qkv[bass.ds(c * P, P), :]

            def out_rows(h):
                return w_o[bass.ds(h * P, P), :]

            def group_loads(pr, g, last):
                order = [(C_Q1, qkv, g * G + 1), (C_O0, out_rows, g * G), (C_Q2, qkv, g * G + 2),
                         (C_O1, out_rows, g * G + 1), (C_Q3, qkv, g * G + 3),
                         (C_V, qkv, g + (HEADS + KV_HEADS + 1)), (C_O2, out_rows, g * G + 2),
                         (C_Q0, qkv, g * G + G), (C_O3, out_rows, g * G + 3),
                         (C_K, qkv, g + (HEADS + 2))]
                for k, source, index in order:
                    if last and k in (C_V, C_Q0, C_K):
                        continue
                    if last:
                        load(pr, group_chunk(k, last) + g * PER_GROUP, source(index))
                    else:
                        load(pr, group_chunk(k, last), source(index), g)

            with sp.Fori(0, PAIRS) as pr:
                load(pr, W_AG, w_ag, cols=HT * AG)
                load(pr, W_T0, w_ffn[0:P, :])
                sp.wait_ge(s_out, pr * (16 * TT) + 16)
                for tt in range(TT):
                    sp.dma_start(acc[:, tt, :], x[bass.ds(pr * PT + tt * P, P), :]).then_inc(s_x[tt // 2], 16)
                load(pr, W_T1, w_ffn[P:2 * P, :])
                load(pr, W_LORA, w_lora, rows=LK)
                for k, t in ((W_T3, 3), (W_T2, 2), (W_T4, 4), (W_T5, 5), (W_T6, 6), (W_T7, 7)):
                    load(pr, k, w_ffn[t * P:(t + 1) * P, :])
                load(pr, W_K0, qkv(HEADS))
                load(pr, W_V0, qkv(HEADS + KV_HEADS))
                load(pr, W_Q0, qkv(0))
                load(pr, W_K1, qkv(HEADS + 1))
                with sp.Fori(0, KV_HEADS - 1) as g:
                    group_loads(pr, g, False)
                group_loads(pr, KV_HEADS - 1, True)
                for tt in range(TT):
                    sp.wait_ge(s_acc, burst_base(pr, BURSTS - 1) + (tt + 1) * HALVES)
                    sp.dma_start(out[bass.ds(pr * PT + tt * P, P), :], acc[:, tt, :]).then_inc(s_out, 16)
            sp.wait_ge(s_out, 16 * TT * PAIRS + 16)

        @block.tensor
        def _(pe):
            def product(to, st, mv, start, stop):
                (st_hi, st_lo), (mv_hi, mv_lo) = st, mv
                pe.matmul(to, st_hi, mv_hi, start=start, stop=False)
                pe.matmul(to, st_hi, mv_lo, start=False, stop=False)
                return pe.matmul(to, st_lo, mv_hi, start=False, stop=stop)

            def xs(ht, a, b):
                return x_hi[:, ht, a:b], x_lo[:, ht, a:b]

            def cut(pair, a, b):
                return pair[0][:, a:b], pair[1][:, a:b]

            def project(to, w, b, tiles=range(HT)):
                for ht in tiles:
                    last = product(to, cut(w, ht * P, (ht + 1) * P), xs(ht, b * SEQ, (b + 1) * SEQ),
                                   ht == 0, ht == HT - 1)
                return last

            def burst(b, pr, g, tiles, left, weights, extra=None):
                for r in tiles:
                    tt, half = r // HALVES, r % HALVES
                    if r >= 2:
                        pe.wait_ge(s_acc, burst_base(pr, b, g) + (r - 1))
                    to = (ps_q, ps_kv)[r % 2][:, :]
                    n = len(weights) + (extra is not None)
                    for i, w in enumerate(weights):
                        last = product(to, left(i, tt * P, (tt + 1) * P), cut(w, half * 512, half * 512 + 512),
                                       i == 0, i == n - 1)
                    if extra is not None:
                        last = product(to, (at_hi[0:LK, 0, tt * P:(tt + 1) * P], at_lo[0:LK, 0, tt * P:(tt + 1) * P]),
                                       (extra[0][0:LK, half * 512:half * 512 + 512],
                                        extra[1][0:LK, half * 512:half * 512 + 512]), False, True)
                    last.then_inc(s_burst, 1)

            def ats(i, a, b):
                return at_hi[:, i, a:b], at_lo[:, i, a:b]

            def ffn_left(m):
                return lambda i, a, b: xs(2 * m + i, a, b)

            def before_groups(pr):
                for tt in range(TT + 1):
                    if tt < TT:
                        pe.wait_ge(s_xn, pr * TT + tt + 1)
                        banks = ((ps_t0, ps_t1), (ps_b, ps_c))[tt % 2]
                        for half in range(2):
                            for i in range(4):
                                ht = 4 * half + i
                                last = pe.transpose(banks[half][:, i * P:(i + 1) * P],
                                                    normed[tt % 2][:, ht * P:(ht + 1) * P], ident[:, :])
                            last.then_inc(s_xt, 1)
                    if tt >= 1:
                        t = tt - 1
                        pe.wait_ge(s_x_lo, pr * (2 * TT) + 2 * (t + 1))
                        if t == 0:
                            pe.wait_ge(s_w_lo, chunk(pr, W_AG) + 2)
                        pe.wait_ge(s_ag_out, pr * TT + t + 1)
                        for ht in range(HT):
                            last = product(ps_a[:, 0:AG], xs(ht, t * P, (t + 1) * P),
                                           cut(wq(0), ht * AG, (ht + 1) * AG), ht == 0, ht == HT - 1)
                        last.then_inc(s_ag, 1)
                        if t == 0:
                            pe.wait_ge(s_w_lo, chunk(pr, W_T1) + 2)
                        burst(0, pr, 0, range(2 * t, 2 * t + 2), ffn_left(0), [wo(0), wo(1)])
                pe.wait_ge(s_w_lo, chunk(pr, W_T2) + 2)
                pe.wait_ge(s_acc, burst_base(pr, 1))
                burst(1, pr, 0, range(BTILES), ffn_left(1), [wq(0), wq(1)])

                pe.wait_ge(s_u, pr + 1)
                settled(pe)
                for half, to in enumerate((ps_t0, ps_t1)):
                    for i in range(4):
                        last = pe.transpose(to[0:R, i * P:(i + 1) * P], u_mask[:, 4 * half + i, :], ident[:, :])
                    last.then_inc(s_ut, 1)
                pe.wait_ge(s_w_lo, chunk(pr, W_T5) + 2)
                pe.wait_ge(s_u_lo, pr * 2 + 2)
                pe.wait_ge(s_acc, burst_base(pr, 2))
                burst(2, pr, 0, range(BTILES), ffn_left(2), [wo(0), wo(1)], extra=wkv)
                pe.wait_ge(s_w_lo, chunk(pr, W_T7) + 2)
                pe.wait_ge(s_acc, burst_base(pr, 3))
                burst(3, pr, 0, range(BTILES), ffn_left(3), [wq(0), wq(1)])

                pe.wait_ge(s_w_lo, chunk(pr, W_K0) + 2)
                pe.wait_ge(s_acc, burst_base(pr, 4))
                project(ps_kv[:, :], wkv, 0).then_inc(s_kv, 1)
                project(ps_q[:, :], wkv, 1).then_inc(s_kv, 1)
                pe.wait_ge(s_w_lo, chunk(pr, W_V0) + 2)
                project(ps_t0[:, :], wo(0), 0).then_inc(s_kv, 1)
                project(ps_t1[:, :], wo(0), 1).then_inc(s_kv, 1)
                pe.wait_ge(s_kv_out, group(pr, 0) * 4 + 2)
                pe.wait_ge(s_w_lo, chunk(pr, W_Q0) + 2)
                project(ps_q[:, :], wq(0), 0).then_inc(s_q, 1)
                pe.wait_ge(s_kv_out, group(pr, 0) * 4 + 4)
                values((ps_kv, ps_t0))

            def values(banks):
                for b, to in enumerate(banks):
                    for i in range(QT):
                        last = pe.transpose(to[:, i * P:(i + 1) * P],
                                            next_v[:, b * SEQ + i * P:b * SEQ + (i + 1) * P], ident[:, :])
                    last.then_inc(s_vt, 1)

            def transposes(pr, g, n):
                pe.wait_ge(s_probs, unit(pr, g, n) + 1)
                for to, tiles in ((ps_t0, [(0, i) for i in range(4)]),
                                  (ps_t1, [(1, 1), (1, 2), (1, 3), (3, 3)]), (ps_o, [(2, 2), (2, 3)])):
                    if to is ps_o:
                        pe.wait_ge(s_at_lo, unit(pr, g, n) + 1)
                    for c, (j, i) in enumerate(tiles):
                        last = pe.transpose(to[:, c * P:(c + 1) * P],
                                            probs[:, OFF[i] + j * P:OFF[i] + (j + 1) * P], ident[:, :])
                    last.then_inc(s_pt, 1)

            def scores(pr, g, n):
                b = n % 2
                if n == 0:
                    pe.wait_ge(s_k_lo, group(pr, g) + 1)
                pe.wait_ge(s_q_lo, unit(pr, g, n) + 1)
                for i in (3, 2, 0, 1):
                    keys = slice(b * SEQ, b * SEQ + (i + 1) * P)
                    last = product(score_bank[i], (q_hi[:, i * P:(i + 1) * P], q_lo[:, i * P:(i + 1) * P]),
                                   (k_hi[:, keys], k_lo[:, keys]), True, True)
                    if i != 0:
                        last.then_inc(s_scores, 1)

            def attend(pr, g, n):
                b = n % 2
                if n == 0:
                    pe.wait_ge(s_v_lo, (group(pr, g) + 1) * 2)
                pe.wait_ge(s_pt_lo, unit(pr, g, n) * 3 + 3)
                for j in (0, 1, 3, 2):
                    width = SEQ - j * P
                    tile = slice(b * SEQ + j * P, b * SEQ + (j + 1) * P)
                    last = product(ps_o[:, j * P:SEQ], (v_hi[:, tile], v_lo[:, tile]),
                                   (pt_hi[:, TOFF[j]:TOFF[j] + width], pt_lo[:, TOFF[j]:TOFF[j] + width]),
                                   j == 0, j == 2)
                last.then_inc(s_o, 1)

            def next_queries(pr, g, n, last_group):
                head = (n + 1) // 2
                if n % 2:
                    name = (None, C_Q1, C_Q2, C_Q3, C_Q0)[head]
                    k = group_chunk(name, last_group) + (g * PER_GROUP if last_group else 0)
                    pe.wait_ge(s_w_lo, chunk(pr, k, 0 if last_group else g) + 2)
                last = project(ps_q[:, :], wq(head % 2), (n + 1) % 2)
                last.then_inc(s_q, 1)

            def next_keys_values(pr, g, n):
                if n == 0:
                    pe.wait_ge(s_w_lo, chunk(pr, BEFORE - 1, g) + 2)
                    pe.wait_ge(s_v_lo, (group(pr, g) + 1) * 2)
                if n == 4:
                    pe.wait_ge(s_w_lo, chunk(pr, BEFORE + C_V, g) + 2)
                if n % 2 == 0:
                    pe.wait_ge(s_kv_out, (group(pr, g) + 1) * 4 + n // 2)
                last = project(ps_kv[:, :], wkv, (n // 2) % 2, range(4 * (n % 2), 4 * (n % 2) + 4))
                if n % 2:
                    last.then_inc(s_kv, 1)

            def heads_burst(pr, g, which, part, last_group):
                b = FFN_BURSTS + which
                if part == 0:
                    k = group_chunk((C_O1, C_O3)[which], last_group) + (g * PER_GROUP if last_group else 0)
                    pe.wait_ge(s_w_lo, chunk(pr, k, 0 if last_group else g) + 2)
                    pe.wait_ge(s_acc, burst_base(pr, b, g))
                    if not (last_group and which == 1):
                        pe.wait_ge(s_q_lo, unit(pr, g, 6 + 3 * which))
                    if not last_group:
                        pe.wait_ge(s_kv_out, (group(pr, g) + 1) * 4 + 2 + 2 * which)
                pe.wait_ge(s_at_lo, unit(pr, g, 4 * which + 2 + part) + 2)
                burst(b, pr, g, range(part * BTILES // 2, (part + 1) * BTILES // 2), ats,
                             [wo(0), wo(1)])

            def one_group(pr, g, last_group):
                for n in range(UNITS):
                    if n:
                        transposes(pr, g, n - 1)
                    scores(pr, g, n)
                    if n < UNITS - 1 or not last_group:
                        if n in (0, 5):
                            pe.wait_ge(s_acc, burst_base(pr, FFN_BURSTS + (n > 0), g))
                        next_queries(pr, g, n, last_group)
                    if n:
                        attend(pr, g, n - 1)
                    if n == 4:
                        heads_burst(pr, g, 0, 0, last_group)
                        heads_burst(pr, g, 0, 1, last_group)
                    if not last_group:
                        if n == 4:
                            pe.wait_ge(s_acc, burst_base(pr, FFN_BURSTS + 1, g))
                        next_keys_values(pr, g, n)
                transposes(pr, g, UNITS - 1)
                heads_burst(pr, g, 1, 0, last_group)
                attend(pr, g, UNITS - 1)
                if not last_group:
                    pe.wait_ge(s_acc, burst_base(pr, FFN_BURSTS + 1, g) + BTILES // 2)
                    pe.wait_ge(s_kv_out, (group(pr, g) + 1) * 4 + 4)
                    values((ps_q, ps_kv))
                    pe.wait_ge(s_v_lo, (group(pr, g) + 2) * 2)
                heads_burst(pr, g, 1, 1, last_group)

            pe.sem_inc(s_burst, 1)
            pe.wait_ge(s_const, 64)
            with pe.Fori(0, PAIRS) as pr:
                before_groups(pr)
                with pe.Fori(0, KV_HEADS - 1) as g:
                    one_group(pr, g, False)
                one_group(pr, KV_HEADS - 1, True)

        def weight_of(k, last):
            return {C_Q1: wq(1), C_O0: wo(0), C_Q2: wq(0), C_O1: wo(1), C_Q3: wq(1), C_V: wkv,
                    C_O2: wo(0), C_Q0: wq(0), C_O3: wo(1), C_K: wkv}[k]

        SPLIT_IN = {0: [C_Q1], 1: [C_O0, C_Q2], 2: [C_O1], 3: [C_Q3], 4: [C_V], 5: [C_O2, C_Q0],
                    6: [C_O3], 7: [], None: [C_K]}

        def group_splits(n, last):
            return [k for k in SPLIT_IN[n] if not (last and k in (C_V, C_Q0, C_K))]

        @block.scalar
        def _(act):
            def high(to, source, signal):
                nc.scalar.activation(to, source, ACT.Copy).then_inc(signal, 1)

            def weights(pr, k, to, g=0, rows=P, cols=HIDDEN):
                slot = k % 2
                loaded = pr * (16 * ((CHUNKS + 1 - slot) // 2)) + g * (16 * PER_GROUP // 2) + 16 * (k // 2 + 1)
                act.wait_ge(s_loaded[slot], loaded)
                high(to[0][0:rows, 0:cols], stage[0:rows, slot, 0:cols], s_w_hi)

            def group_weights(pr, g, n, last_group):
                for k in group_splits(n, last_group):
                    if k in (C_Q1, C_Q2, C_Q3, C_Q0):
                        done = {C_Q1: 1, C_Q2: 2, C_Q3: 4, C_Q0: 6}[k]
                        act.wait_ge(s_q, unit(pr, g, 0) + done)
                    elif k in (C_O0, C_O1, C_O2, C_O3):
                        b = FFN_BURSTS + (k in (C_O2, C_O3))
                        act.wait_ge(s_burst, burst_base(pr, b, g) + 1)
                    else:
                        act.wait_ge(s_kv, (group(pr, g) + 1) * 4 + {C_V: 2, C_K: 4}[k])
                    if last_group:
                        weights(pr, group_chunk(k, True) + g * PER_GROUP, weight_of(k, True))
                    else:
                        weights(pr, group_chunk(k, False), weight_of(k, False), g)

            def transposed(pr, g, n):
                for i, (ps, at, width) in enumerate(t_banks):
                    act.wait_ge(s_pt, unit(pr, g, n) * 3 + i + 1)
                    high(pt_hi[:, at:at + width], ps[:, 0:width], s_pt_hi)

            def exponentials(pr, g, n):
                for c, i in enumerate((3, 2, 0, 1)):
                    act.wait_ge(s_neg_max, unit(pr, g, n) * QT + c + 1)
                    tile = probs[:, OFF[i]:OFF[i] + (i + 1) * P]
                    nc.scalar.activation(tile, tile, ACT.Exp, bias=neg_max[:, i:i + 1], scale=-1.0,
                                         accum_out=row_sum[:, i:i + 1]).then_inc(s_exp, 1)

            def queries(pr, g, n):
                act.wait_ge(s_q, unit(pr, g, n) + 1)
                high(q_hi[:, :], ps_q[:, :], s_q_hi)

            def outputs(pr, g, n):
                act.wait_ge(s_o, unit(pr, g, n) + 1)
                high(at_hi[:, (n // 2) % 2, (n % 2) * SEQ:(n % 2 + 1) * SEQ], ps_o[:, :], s_at_hi)

            def keys(pr, gt):
                act.wait_ge(s_kv_out, gt * 4 + 2)
                high(k_hi[:, :], next_k[:, :], s_k_hi)

            def values(gt, banks):
                for b, ps in enumerate(banks):
                    act.wait_ge(s_vt, gt * 2 + b + 1)
                    high(v_hi[:, b * SEQ:(b + 1) * SEQ], ps[:, :], s_v_hi)

            def root_of(pr, q):
                act.wait_ge(s_var, pr * (TT // 2) + q + 1)
                nc.scalar.activation(root[:, :], root[:, :], ACT.Sqrt).then_inc(s_std, 1)

            def one_group(pr, g, last_group):
                for n in range(UNITS):
                    if n:
                        transposed(pr, g, n - 1)
                    exponentials(pr, g, n)
                    group_weights(pr, g, n, last_group)
                    if n == UNITS - 1 and not last_group:
                        keys(pr, group(pr, g) + 1)
                    if n < UNITS - 1 or not last_group:
                        queries(pr, g, n + 1)
                    if n:
                        outputs(pr, g, n - 1)
                transposed(pr, g, UNITS - 1)
                group_weights(pr, g, None, last_group)
                outputs(pr, g, UNITS - 1)
                if not last_group:
                    values(group(pr, g) + 1, (ps_q, ps_kv))

            with act.Fori(0, PAIRS) as pr:
                act.wait_ge(s_burst, burst_base(pr, 0) + 1)
                weights(pr, W_AG, wq(0), cols=HT * AG)
                root_of(pr, 0)
                weights(pr, W_T0, wo(0))
                weights(pr, W_T1, wo(1))
                for tt in range(TT):
                    if tt % 2 == 0 and tt // 2 + 1 < TT // 2:
                        root_of(pr, tt // 2 + 1)
                    for half in range(2):
                        act.wait_ge(s_xt, pr * (2 * TT) + 2 * tt + half + 1)
                        ps = ((ps_t0, ps_t1), (ps_b, ps_c))[tt % 2][half]
                        high(x_hi[:, 4 * half:4 * half + 4, tt * P:(tt + 1) * P],
                             ps[:, :].rearrange("p (h t) -> p h t", h=4), s_x_hi)
                    if tt == 2:
                        weights(pr, W_LORA, wkv, rows=LK)
                    if tt == 4:
                        weights(pr, W_T3, wq(1))
                act.wait_ge(s_ag, pr * TT + TT)
                weights(pr, W_T2, wq(0))
                act.wait_ge(s_gate, pr + 1)
                nc.scalar.activation(gate_buf[:, 1], gate_buf[:, 1], ACT.Exp).then_inc(s_gate_exp, 1)
                act.wait_ge(s_burst, burst_base(pr, 1) + 1)
                weights(pr, W_T4, wo(0))
                weights(pr, W_T5, wo(1))
                for half, ps in enumerate((ps_t0, ps_t1)):
                    act.wait_ge(s_ut, pr * 2 + half + 1)
                    high(at_hi[0:R, 0, half * 512:(half + 1) * 512], ps[0:R, :], s_u_hi)
                act.wait_ge(s_burst, burst_base(pr, 2) + 1)
                weights(pr, W_T6, wq(0))
                weights(pr, W_T7, wq(1))
                act.wait_ge(s_burst, burst_base(pr, 3) + 1)
                weights(pr, W_K0, wkv)
                weights(pr, W_V0, wo(0))
                act.wait_ge(s_burst, burst_base(pr, 4) + 1)
                weights(pr, W_Q0, wq(0))
                act.wait_ge(s_kv, group(pr, 0) * 4 + 2)
                weights(pr, W_K1, wkv)
                keys(pr, group(pr, 0))
                queries(pr, 0, 0)
                values(group(pr, 0), (ps_kv, ps_t0))
                with act.Fori(0, KV_HEADS - 1) as g:
                    one_group(pr, g, False)
                one_group(pr, KV_HEADS - 1, True)

        @block.vector
        def _(dve):
            links = [0]

            def link(pr, ins):
                links[0] += 1
                ins.then_inc(s_link, 1)
                dve.wait_ge(s_link, pr * LINKS + links[0])

            def low(to, source, high, signal):
                nc.vector.tensor_tensor(to, source, high.bitcast(F32), ALU.subtract).then_inc(signal, 1)

            def weights(pr, k, to, g=0, rows=P, cols=HIDDEN):
                dve.wait_ge(s_w_hi, chunk(pr, k, g) + 1)
                low(to[1][0:rows, 0:cols], stage[0:rows, k % 2, 0:cols], to[0][0:rows, 0:cols], s_w_lo)

            def group_weights(pr, g, n, last_group):
                for k in group_splits(n, last_group):
                    if last_group:
                        weights(pr, group_chunk(k, True) + g * PER_GROUP, weight_of(k, True))
                    else:
                        weights(pr, group_chunk(k, False), weight_of(k, False), g)

            def transposed(pr, g, n):
                for i, (ps, at, width) in enumerate(t_banks):
                    dve.wait_ge(s_pt_hi, unit(pr, g, n) * 3 + i + 1)
                    low(pt_lo[:, at:at + width], ps[:, 0:width], pt_hi[:, at:at + width], s_pt_lo)

            def bias_of(head):
                nc.vector.tensor_scalar(head_bias[:, :], dist[:, :], slopes[:, bass.ds(head, 1)], None,
                                        ALU.mult).then_inc(s_bias, 1)

            def maxima(pr, g, n):
                if n % 2 == 0:
                    dve.wait_ge(s_bias, pr * HEADS + g * G + n // 2 + 1)
                for c, i in enumerate((3, 2, 0, 1)):
                    if i != 1:
                        dve.wait_ge(s_scores, unit(pr, g, n) * 3 + c + 1)
                        settled(dve)
                    nc.vector.tensor_tensor_reduce(
                        out=probs[:, OFF[i]:OFF[i] + (i + 1) * P], in0=score_bank[i],
                        in1=head_bias[:, SEQ - (i + 1) * P:SEQ], scale=-SCALE, scalar=3e38,
                        op0=ALU.add, op1=ALU.min, accum_out=neg_max[:, i:i + 1]).then_inc(s_neg_max, 1)

            def normalise(pr, g, n):
                dve.wait_ge(s_exp, unit(pr, g, n) * QT + QT)
                nc.vector.reciprocal(row_inv[:, :], row_sum[:, :]).then_inc(s_inv, 1)
                dve.wait_ge(s_inv, unit(pr, g, n) + 1)
                for i in range(QT):
                    tile = probs[:, OFF[i]:OFF[i] + (i + 1) * P]
                    last = nc.vector.tensor_scalar(tile, tile, row_inv[:, i:i + 1], None, ALU.mult)
                last.then_inc(s_probs, 1)

            def queries(pr, g, n):
                dve.wait_ge(s_q_hi, unit(pr, g, n) + 1)
                low(q_lo[:, :], ps_q[:, :], q_hi[:, :], s_q_lo)

            def outputs(pr, g, n):
                dve.wait_ge(s_at_hi, unit(pr, g, n) + 1)
                at = (slice(None), (n // 2) % 2, slice((n % 2) * SEQ, (n % 2 + 1) * SEQ))
                low(at_lo[at], ps_o[:, :], at_hi[at], s_at_lo)

            def copy_piece(gt, piece, ps):
                dve.wait_ge(s_kv, gt * 4 + piece + 1)
                to = (next_k, next_v)[piece // 2]
                nc.vector.tensor_copy(to[:, (piece % 2) * SEQ:(piece % 2 + 1) * SEQ], ps[:, :]).then_inc(s_kv_out, 1)

            def keys(gt):
                dve.wait_ge(s_k_hi, gt + 1)
                low(k_lo[:, :], next_k[:, :], k_hi[:, :], s_k_lo)

            def values(gt, banks):
                for b, ps in enumerate(banks):
                    dve.wait_ge(s_v_hi, gt * 2 + b + 1)
                    low(v_lo[:, b * SEQ:(b + 1) * SEQ], ps[:, :], v_hi[:, b * SEQ:(b + 1) * SEQ], s_v_lo)

            def add(pr, b, tiles, g=0):
                for r in tiles:
                    dve.wait_ge(s_burst, burst_base(pr, b, g) + r + 2)
                    to = acc[:, r // HALVES, (r % HALVES) * 512:(r % HALVES + 1) * 512]
                    nc.vector.tensor_tensor(to, (ps_q, ps_kv)[r % 2][:, :], to, ALU.add).then_inc(s_acc, 1)

            def inverse_deviation(pr, q):
                dve.wait_ge(s_x[q], (pr + 1) * 32)
                for i in range(2):
                    for half in range(2):
                        last = nc.vector.bn_stats(stats[:, i, half, :], acc[:, 2 * q + i, half * 512:(half + 1) * 512])
                link(pr, last)
                settled(dve)
                mom = moments[:, q % 2]
                for i in range(2):
                    last = nc.vector.bn_aggr(mom[:, i, :], stats[:, i])
                link(pr, last)
                r = rstd[:, 2 * q:2 * q + 2]
                nc.vector.tensor_scalar(root[:, :], mom[:, :, 1], EPS, None, ALU.add).then_inc(s_var, 1)
                dve.wait_ge(s_std, pr * (TT // 2) + q + 1)
                link(pr, nc.vector.reciprocal(r, root[:, :]))
                link(pr, nc.vector.scalar_tensor_tensor(newton[:, :], mom[:, :, 1], EPS, r, ALU.add, ALU.mult))
                link(pr, nc.vector.tensor_tensor(newton[:, :], newton[:, :], r, ALU.mult))
                link(pr, nc.vector.tensor_scalar(newton[:, :], newton[:, :], -0.5, 1.5, ALU.mult, ALU.add))
                link(pr, nc.vector.tensor_tensor(r, r, newton[:, :], ALU.mult))

            def normalised(pr, tt):
                if tt >= 2:
                    dve.wait_ge(s_xt, pr * (2 * TT) + 2 * (tt - 1))
                nc.vector.tensor_scalar(normed[tt % 2], acc[:, tt, :], moments[:, (tt // 2) % 2, tt % 2, 0:1],
                                        rstd[:, tt:tt + 1], ALU.subtract, ALU.mult).then_inc(s_xn, 1)

            def gate_scores(pr):
                z, d = gate_buf[:, 0], gate_buf[:, 1]
                link(pr, nc.vector.tensor_tensor(z, ag_out[:, :, R:AG],
                                                 gbias[:, :].unsqueeze(1).to_broadcast([P, TT, E]), ALU.add))
                link(pr, nc.vector.tensor_reduce(gate_col[:, 0], z, AX.X, ALU.max))
                nc.vector.tensor_tensor(d, z, gate_col[:, 0].unsqueeze(2).to_broadcast([P, TT, E]),
                                        ALU.subtract).then_inc(s_gate, 1)

            def gate_masks(pr):
                p = gate_buf[:, 0]
                e, inv, top, rtop, weight, p01, p012 = gate_buf[:, 1], *(gate_col[:, i] for i in range(1, 7))
                total = gate_col[:, 0]
                dve.wait_ge(s_gate_exp, pr + 1)
                link(pr, nc.vector.tensor_reduce(total, e, AX.X, ALU.add))
                link(pr, nc.vector.reciprocal(inv, total))
                link(pr, nc.vector.tensor_tensor(p, e, inv.unsqueeze(2).to_broadcast([P, TT, E]), ALU.mult))
                nc.vector.tensor_tensor(p01, p[:, :, 0], p[:, :, 1], ALU.max)
                link(pr, nc.vector.tensor_reduce(top, p, AX.X, ALU.max))
                nc.vector.tensor_tensor(p012, p01, p[:, :, 2], ALU.max)
                link(pr, nc.vector.reciprocal(rtop, top))
                link(pr, nc.vector.tensor_tensor(weight, top, rtop, ALU.mult))
                chosen = [gate_col[:, 7 + i] for i in range(3)]
                for to, before in zip(chosen, (p[:, :, 0], p01, p012)):
                    last = nc.vector.tensor_tensor(to, before, top, ALU.is_lt)
                link(pr, last)
                for to in chosen:
                    last = nc.vector.tensor_tensor(to, to, weight, ALU.mult)
                link(pr, last)
                lows = (0,) + RANKS[:-1]
                for low_rank, rank, w in zip(lows, RANKS, [weight] + chosen):
                    last = nc.vector.tensor_tensor(
                        u_mask[:, :, low_rank:rank], ag_out[:, :, low_rank:rank],
                        w.unsqueeze(2).to_broadcast([P, TT, rank - low_rank]), ALU.mult)
                last.then_inc(s_u, 1)

            def one_group(pr, g, last_group):
                for n in range(UNITS):
                    if n:
                        transposed(pr, g, n - 1)
                    maxima(pr, g, n)
                    normalise(pr, g, n)
                    if n % 2 and (n < UNITS - 1 or not last_group):
                        bias_of(g * G + (n + 1) // 2)
                    group_weights(pr, g, n, last_group)
                    if n == UNITS - 1 and not last_group:
                        keys(group(pr, g) + 1)
                    if n < UNITS - 1 or not last_group:
                        queries(pr, g, n + 1)
                    if n:
                        outputs(pr, g, n - 1)
                    if n == 4:
                        add(pr, FFN_BURSTS, range(BTILES), g)
                    if n % 2 and not last_group:
                        copy_piece(group(pr, g) + 1, n // 2, ps_kv)
                transposed(pr, g, UNITS - 1)
                group_weights(pr, g, None, last_group)
                add(pr, FFN_BURSTS + 1, range(BTILES // 2), g)
                outputs(pr, g, UNITS - 1)
                if not last_group:
                    values(group(pr, g) + 1, (ps_q, ps_kv))
                add(pr, FFN_BURSTS + 1, range(BTILES // 2, BTILES), g)

            dve.sem_inc(s_w_lo, 1)
            dve.sem_inc(s_at_lo, 1)
            dve.sem_inc(s_ag_out, 1)
            dve.wait_ge(s_const, 64)
            with dve.Fori(0, PAIRS) as pr:
                weights(pr, W_AG, wq(0), cols=HT * AG)
                inverse_deviation(pr, 0)
                normalised(pr, 0)
                weights(pr, W_T0, wo(0))
                weights(pr, W_T1, wo(1))
                for tt in range(TT + 1):
                    if tt < TT:
                        if tt % 2 == 0 and tt // 2 + 1 < TT // 2:
                            inverse_deviation(pr, tt // 2 + 1)
                        if tt + 1 < TT:
                            normalised(pr, tt + 1)
                        for half in range(2):
                            dve.wait_ge(s_x_hi, pr * (2 * TT) + 2 * tt + half + 1)
                            ps = ((ps_t0, ps_t1), (ps_b, ps_c))[tt % 2][half]
                            at = (slice(None), slice(4 * half, 4 * half + 4), slice(tt * P, (tt + 1) * P))
                            low(x_lo[at], ps[:, :].rearrange("p (h t) -> p h t", h=4), x_hi[at], s_x_lo)
                        if tt == 2:
                            weights(pr, W_LORA, wkv, rows=LK)
                        if tt == 4:
                            weights(pr, W_T3, wq(1))
                    if tt >= 1:
                        dve.wait_ge(s_ag, pr * TT + tt)
                        nc.vector.tensor_copy(ag_out[:, tt - 1, :], ps_a[:, 0:AG]).then_inc(s_ag_out, 1)
                        if tt == TT:
                            weights(pr, W_T2, wq(0))
                        add(pr, 0, range(2 * (tt - 1), 2 * tt))
                nc.vector.memset(at_hi[R:LK, 0, :].bitcast(F32), 1.0)
                nc.vector.memset(at_lo[R:LK, 0, :].bitcast(F32), 0.0)
                add(pr, 1, range(0, 2))
                gate_scores(pr)
                add(pr, 1, range(2, 5))
                gate_masks(pr)
                add(pr, 1, range(5, 8))
                weights(pr, W_T4, wo(0))
                add(pr, 1, range(8, 10))
                weights(pr, W_T5, wo(1))
                add(pr, 1, range(10, BTILES))
                for half, ps in enumerate((ps_t0, ps_t1)):
                    dve.wait_ge(s_u_hi, pr * 2 + half + 1)
                    low(at_lo[0:R, 0, half * 512:(half + 1) * 512], ps[0:R, :],
                        at_hi[0:R, 0, half * 512:(half + 1) * 512], s_u_lo)
                weights(pr, W_T6, wq(0))
                add(pr, 2, range(0, 2))
                weights(pr, W_T7, wq(1))
                add(pr, 2, range(2, BTILES))
                weights(pr, W_K0, wkv)
                add(pr, 3, range(0, 2))
                weights(pr, W_V0, wo(0))
                add(pr, 3, range(2, BTILES))
                weights(pr, W_Q0, wq(0))
                copy_piece(group(pr, 0), 0, ps_kv)
                copy_piece(group(pr, 0), 1, ps_q)
                weights(pr, W_K1, wkv)
                keys(group(pr, 0))
                copy_piece(group(pr, 0), 2, ps_t0)
                copy_piece(group(pr, 0), 3, ps_t1)
                bias_of(0)
                queries(pr, 0, 0)
                values(group(pr, 0), (ps_kv, ps_t0))
                assert links[0] == LINKS, links
                with dve.Fori(0, KV_HEADS - 1) as g:
                    one_group(pr, g, False)
                one_group(pr, KV_HEADS - 1, True)


def constants():
    row = np.arange(P)[:, None]
    rel = row - (np.arange(SEQ)[None, :] - (SEQ - P))
    dist = np.where(rel >= 0, np.sqrt(np.maximum(rel, 0).astype(np.float32)), np.float32(MASKED))
    slopes = np.float32(2.0 ** (-8.0 / HEADS)) ** np.arange(1, HEADS + 1, dtype=np.float32)
    rows = np.broadcast_to(-slopes.astype(np.float64) / SCALE, (P, HEADS))
    return np.concatenate([dist, np.eye(P), rows], axis=1).astype(np.float32)


def kernel(L0_attn_hidden_states, L0_attn_w_qkv, L0_attn_w_o, L0_ffn_W, L0_ffn_b, L0_ffn_A, L0_ffn_B,
           L0_ffn_gate_w, L0_ffn_gate_b):
    import concourse.bacc as bacc
    from concourse.bass_utils import run_bass_kernel_spmd

    f = np.ascontiguousarray
    shape = L0_attn_hidden_states.shape
    w_qkv = np.asarray(L0_attn_w_qkv).reshape(HT, P, -1, P).transpose(2, 1, 0, 3).reshape(-1, HIDDEN)
    ag = np.concatenate([np.asarray(L0_ffn_A), np.asarray(L0_ffn_gate_w)]).T
    arrays = {
        "x": f(np.asarray(L0_attn_hidden_states).reshape(TOKENS, HIDDEN)),
        "w_qkv": f(w_qkv),
        "w_o": f(L0_attn_w_o),
        "w_ffn": f(np.asarray(L0_ffn_W).T),
        "w_ag": f(ag.reshape(HT, P, AG).transpose(1, 0, 2).reshape(P, HT * AG)),
        "w_lora": f(np.concatenate([np.asarray(L0_ffn_B).T, np.asarray(L0_ffn_b)[None, :]])),
        "gate_b": f(L0_ffn_gate_b),
        "consts": constants(),
    }
    nc = bacc.Bacc("TRN2", target_bir_lowering=False, num_devices=1)
    args = [nc.dram_tensor(n, a.shape, F32, kind="ExternalInput").ap() for n, a in arrays.items()]
    out = nc.dram_tensor("out", (TOKENS, HIDDEN), F32, kind="ExternalOutput").ap()
    block_program(nc, *args, out)
    result = run_bass_kernel_spmd(nc, [arrays], core_ids=[0])
    return result.results[0]["out"].reshape(shape)
```

```python
from contextlib import ExitStack

import numpy as np

import concourse.bass as bass
from concourse import mybir

ALU = mybir.AluOpType
ACT = mybir.ActivationFunctionType
AX = mybir.AxisListType
F32 = mybir.dt.float32
F32R = mybir.dt.float32r

P = 128
HIDDEN = 1024
HEADS = 32
KV_HEADS = 8
G = HEADS // KV_HEADS
D = 128
BATCH = 4
SEQ = 512
TOKENS = BATCH * SEQ
SCALE = float(D) ** -0.5
EPS = 1e-5
RANKS = (8, 16, 32, 64)
R = max(RANKS)
E = len(RANKS)

PAIRS = BATCH // 2
PT = TOKENS // PAIRS
TT = PT // P
HT = HIDDEN // P
QT = SEQ // P
UNITS = 2 * G
NP = QT * (QT + 1) // 2 * P
HALVES = HIDDEN // 512
BTILES = TT * HALVES
MASKED = 1e36
AG = R + E
LK = R + 1

OFF = [P * (i * (i + 1) // 2) for i in range(QT)]
TOFF = {0: 0, 1: 512, 3: 896, 2: 1024}

W_AG, W_T0, W_T1, W_T2, W_T3, W_LORA, W_T4, W_T5, W_T6, W_T7, W_K0, W_V0, W_Q0, W_K1 = range(14)
BEFORE = 14
C_Q1, C_O0, C_Q2, C_O1, C_Q3, C_V, C_O2, C_Q0, C_O3, C_K = range(10)
PER_GROUP = 10
L_Q1, L_O0, L_Q2, L_O1, L_Q3, L_O2, L_O3 = range(7)
CHUNKS = BEFORE + PER_GROUP * (KV_HEADS - 1) + 7

FFN_BURSTS = HT // 2
BURSTS = FFN_BURSTS + 2 * KV_HEADS
LINKS = 7 * (TT // 2) + 10


def block_program(nc, x, w_qkv, w_o, w_ffn, w_ag, w_lora, gate_b, consts, out):
    with ExitStack() as ctx:
        def sb(name, shape, dt=F32):
            return ctx.enter_context(nc.sbuf_tensor(name, shape, dt))

        def bank(name):
            return ctx.enter_context(nc.psum_tensor(name, [P, 512], F32))

        def sem(name):
            return ctx.enter_context(nc.semaphore(name))

        x_hi = sb("x_hi", [P, HT, PT], F32R)
        x_lo = sb("x_lo", [P, HT, PT], F32R)
        acc = sb("acc", [P, TT, HIDDEN])
        at_hi = sb("at_hi", [P, 2, PT], F32R)
        at_lo = sb("at_lo", [P, 2, PT], F32R)
        wo_hi = sb("wo_hi", [P, 2, HIDDEN], F32R)
        wo_lo = sb("wo_lo", [P, 2, HIDDEN], F32R)
        wq_hi = sb("wq_hi", [P, 2, HIDDEN], F32R)
        wq_lo = sb("wq_lo", [P, 2, HIDDEN], F32R)
        wkv_hi = sb("wkv_hi", [P, HIDDEN], F32R)
        wkv_lo = sb("wkv_lo", [P, HIDDEN], F32R)
        q_hi = sb("q_hi", [P, SEQ], F32R)
        q_lo = sb("q_lo", [P, SEQ], F32R)
        k_hi = sb("k_hi", [P, PT], F32R)
        k_lo = sb("k_lo", [P, PT], F32R)
        v_hi = sb("v_hi", [P, PT], F32R)
        v_lo = sb("v_lo", [P, PT], F32R)
        next_k = sb("next_k", [P, PT])
        next_v = sb("next_v", [P, PT])
        stage = sb("stage", [P, 2, HIDDEN])
        probs = sb("probs", [P, NP])
        pt_hi = sb("pt_hi", [P, NP], F32R)
        pt_lo = sb("pt_lo", [P, NP], F32R)
        dist = sb("dist", [P, SEQ])
        head_bias = sb("head_bias", [P, SEQ])
        ident = sb("ident", [P, P])
        slopes = sb("slopes", [P, HEADS])
        gbias = sb("gbias", [P, E])
        neg_max = sb("neg_max", [P, QT])
        row_sum = sb("row_sum", [P, QT])
        row_inv = sb("row_inv", [P, QT])

        ps_a, ps_b, ps_c = bank("ps_a"), bank("ps_b"), bank("ps_c")
        ps_t0, ps_t1 = bank("ps_t0"), bank("ps_t1")
        ps_o = bank("ps_o")
        ps_q, ps_kv = bank("ps_q"), bank("ps_kv")

        ag_rows = next_v[0:AG, :]
        ag_out = next_k[:, 0:TT * AG].rearrange("p (t a) -> p t a", a=AG)
        small = next_k[:, TT * AG:TT * AG + 48]
        stats = small[:, 0:24].rearrange("p (t h s) -> p t h s", t=2, h=2)
        moments = small[:, 24:32].rearrange("p (g t m) -> p g t m", g=2, t=2)
        rstd, root, newton = small[:, 32:40], small[:, 40:42], small[:, 42:44]
        u_mask = probs[:, 0:TT * R].rearrange("p (t a) -> p t a", a=R)
        gate_buf = probs[:, TT * R:TT * (R + 2 * E)].rearrange("p (k t e) -> p k t e", k=2, e=E)
        gate_col = probs[:, TT * (R + 2 * E):TT * (R + 2 * E + 10)].rearrange("p (k t) -> p k t", t=TT)
        normed = [probs[:, 0:HIDDEN], next_v[:, :]]
        score_bank = {3: ps_c[:, :], 2: ps_b[:, 0:3 * P], 0: ps_a[:, 0:P], 1: ps_a[:, P:3 * P]}

        def t_banks(last_group):
            return [(ps_t0, 0, 512), (ps_t1, 512, 512), (ps_kv if last_group else ps_o, 1024, 256)]

        def ring(b):
            if b == 0:
                return [ps_q, ps_kv]
            if b < FFN_BURSTS:
                return [ps_q, ps_kv, ps_b, ps_c]
            return [ps_kv, ps_b, ps_c, ps_q] if b == FFN_BURSTS else [ps_b, ps_c, ps_q, ps_kv]


        s_const = sem("s_const")
        s_x = [sem(f"s_x{i}") for i in range(TT)]
        s_loaded = [sem("s_loaded0"), sem("s_loaded1")]
        s_w_hi = sem("s_w_hi")
        s_w_lo = sem("s_w_lo")
        s_link = sem("s_link")
        s_var = sem("s_var")
        s_std = sem("s_std")
        s_xn = sem("s_xn")
        s_xt = sem("s_xt")
        s_x_hi = sem("s_x_hi")
        s_x_lo = sem("s_x_lo")
        s_ag = sem("s_ag")
        s_ag_row = sem("s_ag_row")
        s_agt = sem("s_agt")
        s_ag_out = sem("s_ag_out")
        s_gate = sem("s_gate")
        s_gate_exp = sem("s_gate_exp")
        s_u = sem("s_u")
        s_ut = sem("s_ut")
        s_u_hi = sem("s_u_hi")
        s_u_lo = sem("s_u_lo")
        s_acc = sem("s_acc")
        s_burst = sem("s_burst")
        s_kv = sem("s_kv")
        s_kv_out = sem("s_kv_out")
        s_k_hi = sem("s_k_hi")
        s_k_lo = sem("s_k_lo")
        s_vt = sem("s_vt")
        s_v_hi = sem("s_v_hi")
        s_v_lo = sem("s_v_lo")
        s_q = sem("s_q")
        s_q_hi = sem("s_q_hi")
        s_q_lo = sem("s_q_lo")
        s_bias = sem("s_bias")
        s_scores = sem("s_scores")
        s_neg_max = sem("s_neg_max")
        s_exp = sem("s_exp")
        s_inv = sem("s_inv")
        s_probs = sem("s_probs")
        s_pt = sem("s_pt")
        s_pt_hi = sem("s_pt_hi")
        s_pt_lo = sem("s_pt_lo")
        s_o = sem("s_o")
        s_at_hi = sem("s_at_hi")
        s_at_lo = sem("s_at_lo")
        s_out = [sem(f"s_out{i}") for i in range(TT)]
        s_acc_free = sem("s_acc_free")
        s_settled = sem("s_settled")

        def unit(pr, g, n):
            return pr * (KV_HEADS * UNITS) + g * UNITS + n

        def group(pr, g):
            return pr * KV_HEADS + g

        def chunk(pr, k, g=0):
            return pr * CHUNKS + g * PER_GROUP + k

        def group_chunk(k, last):
            if not last:
                return BEFORE + k
            return BEFORE + {C_Q1: L_Q1, C_O0: L_O0, C_Q2: L_Q2, C_O1: L_O1, C_Q3: L_Q3,
                             C_O2: L_O2, C_O3: L_O3}[k]

        def burst_base(pr, b, g=0):
            return pr * (BURSTS * BTILES) + g * (2 * BTILES) + b * BTILES

        def wq(i):
            return wq_hi[:, i, :], wq_lo[:, i, :]

        def wo(i):
            return wo_hi[:, i, :], wo_lo[:, i, :]

        wkv = (wkv_hi[:, :], wkv_lo[:, :])

        block = ctx.enter_context(nc.Block())

        def settled(eng):
            eng.sem_inc(s_settled, 1)

        @block.sync
        def _(sp):
            sp.dma_start(dist[:, :], consts[:, 0:SEQ]).then_inc(s_const, 16)
            sp.dma_start(ident[:, :], consts[:, SEQ:SEQ + P]).then_inc(s_const, 16)
            sp.dma_start(slopes[:, :], consts[:, SEQ + P:SEQ + P + HEADS]).then_inc(s_const, 16)
            sp.dma_start(gbias[:, :], gate_b.partition_broadcast(P)).then_inc(s_const, 16)

            def load(pr, k, source, g=0, rows=P, cols=HIDDEN):
                sp.wait_ge(s_w_lo, chunk(pr, max(k - 1, 0), g) + 1)
                sp.dma_start(stage[0:rows, k % 2, 0:cols], source).then_inc(s_loaded[k % 2], 16)

            def qkv(c):
                return w_qkv[bass.ds(c * P, P), :]

            def out_rows(h):
                return w_o[bass.ds(h * P, P), :]

            def group_loads(pr, g, last):
                order = [(C_Q1, qkv, g * G + 1), (C_O0, out_rows, g * G), (C_Q2, qkv, g * G + 2),
                         (C_O1, out_rows, g * G + 1), (C_Q3, qkv, g * G + 3),
                         (C_V, qkv, g + (HEADS + KV_HEADS + 1)), (C_O2, out_rows, g * G + 2),
                         (C_Q0, qkv, g * G + G), (C_O3, out_rows, g * G + 3),
                         (C_K, qkv, g + (HEADS + 2))]
                for k, source, index in order:
                    if last and k in (C_V, C_Q0, C_K):
                        continue
                    if last:
                        load(pr, group_chunk(k, last) + g * PER_GROUP, source(index))
                    else:
                        load(pr, group_chunk(k, last), source(index), g)

            with sp.Fori(0, PAIRS) as pr:
                load(pr, W_AG, w_ag, cols=HT * AG)
                load(pr, W_T0, w_ffn[0:P, :])
                load(pr, W_T1, w_ffn[P:2 * P, :])
                load(pr, W_T2, w_ffn[2 * P:3 * P, :])
                load(pr, W_T3, w_ffn[3 * P:4 * P, :])
                load(pr, W_LORA, w_lora, rows=LK)
                for k, t in ((W_T4, 4), (W_T5, 5), (W_T6, 6), (W_T7, 7)):
                    load(pr, k, w_ffn[t * P:(t + 1) * P, :])
                load(pr, W_K0, qkv(HEADS))
                load(pr, W_V0, qkv(HEADS + KV_HEADS))
                load(pr, W_Q0, qkv(0))
                load(pr, W_K1, qkv(HEADS + 1))
                with sp.Fori(0, KV_HEADS - 1) as g:
                    group_loads(pr, g, False)
                group_loads(pr, KV_HEADS - 1, True)

        @block.gpsimd
        def _(pool):
            pool.sem_inc(s_acc_free, TT)
            with pool.Fori(0, PAIRS) as pr:
                for tt in range(TT + 1):
                    if tt < TT:
                        pool.wait_ge(s_acc, burst_base(pr, BURSTS - 1) + (tt + 1) * HALVES)
                        pool.dma_start(out[bass.ds(pr * PT + tt * P, P), :], acc[:, tt, :]).then_inc(s_out[tt], 16)
                    if tt:
                        pool.wait_ge(s_out[tt - 1], pr * 16 + 16)
                        pool.sem_inc(s_acc_free, 1)

        @block.tensor
        def _(pe):
            def product(to, st, mv, start, stop):
                (st_hi, st_lo), (mv_hi, mv_lo) = st, mv
                pe.matmul(to, st_hi, mv_hi, start=start, stop=False)
                pe.matmul(to, st_hi, mv_lo, start=False, stop=False)
                return pe.matmul(to, st_lo, mv_hi, start=False, stop=stop)

            def xs(ht, a, b):
                return x_hi[:, ht, a:b], x_lo[:, ht, a:b]

            def cut(pair, a, b):
                return pair[0][:, a:b], pair[1][:, a:b]

            def project(to, w, b, tiles=range(HT)):
                for ht in tiles:
                    last = product(to, cut(w, ht * P, (ht + 1) * P), xs(ht, b * SEQ, (b + 1) * SEQ),
                                   ht == 0, ht == HT - 1)
                return last

            def burst(b, pr, g, tiles, left, weights, extra=None):
                banks = ring(b)
                for r in tiles:
                    tt, half = r // HALVES, r % HALVES
                    if r >= len(banks) or 2 <= b < FFN_BURSTS:
                        pe.wait_ge(s_acc, burst_base(pr, b, g) + (r - len(banks) + 1))
                    elif b == 1 and r < 2:
                        pe.wait_ge(s_acc, burst_base(pr, b, g) + (r - 1))
                    to = banks[r % len(banks)][:, :]
                    n = len(weights) + (extra is not None)
                    for i, w in enumerate(weights):
                        last = product(to, left(i, tt * P, (tt + 1) * P), cut(w, half * 512, half * 512 + 512),
                                       i == 0, i == n - 1)
                    if extra is not None:
                        last = product(to, (at_hi[0:LK, 0, tt * P:(tt + 1) * P], at_lo[0:LK, 0, tt * P:(tt + 1) * P]),
                                       (extra[0][0:LK, half * 512:half * 512 + 512],
                                        extra[1][0:LK, half * 512:half * 512 + 512]), False, True)
                    last.then_inc(s_burst, 1)

            def ats(i, a, b):
                return at_hi[:, i, a:b], at_lo[:, i, a:b]

            def ffn_left(m):
                return lambda i, a, b: xs(2 * m + i, a, b)

            def before_groups(pr):
                for tt in range(TT + 1):
                    if tt < TT:
                        pe.wait_ge(s_xn, pr * TT + tt + 1)
                        banks = ((ps_t0, ps_t1), (ps_b, ps_c))[tt % 2]
                        for half in range(2):
                            for i in range(4):
                                ht = 4 * half + i
                                last = pe.transpose(banks[half][:, i * P:(i + 1) * P],
                                                    normed[tt % 2][:, ht * P:(ht + 1) * P], ident[:, :])
                            last.then_inc(s_xt, 1)
                    if tt >= 1:
                        t = tt - 1
                        pe.wait_ge(s_x_lo, pr * (2 * TT) + 2 * (t + 1))
                        if t == 0:
                            pe.wait_ge(s_w_lo, chunk(pr, W_T1) + 2)
                        burst(0, pr, 0, range(2 * t, 2 * t + 2), ffn_left(0), [wo(0), wo(1)])

                pe.wait_ge(s_w_lo, chunk(pr, W_AG) + 2)
                for b, to in enumerate((ps_a, ps_t0)):
                    for ht in range(HT):
                        last = product(to[0:AG, :], cut(wkv, ht * AG, (ht + 1) * AG),
                                       xs(ht, b * SEQ, (b + 1) * SEQ), ht == 0, ht == HT - 1)
                    last.then_inc(s_ag, 1)
                pe.wait_ge(s_w_lo, chunk(pr, W_T3) + 2)
                burst(1, pr, 0, range(0, 4), ffn_left(1), [wq(0), wq(1)])
                pe.wait_ge(s_ag_row, pr * 2 + 2)
                for half, to in enumerate((ps_a, ps_t1)):
                    for i in range(4):
                        tt = 4 * half + i
                        last = pe.transpose(to[:, i * AG:(i + 1) * AG], ag_rows[:, tt * P:(tt + 1) * P],
                                            ident[0:AG, 0:AG])
                    last.then_inc(s_agt, 1)
                burst(1, pr, 0, range(4, BTILES), ffn_left(1), [wq(0), wq(1)])

                pe.wait_ge(s_u, pr + 1)
                settled(pe)
                for half, to in enumerate((ps_t0, ps_t1)):
                    for i in range(4):
                        last = pe.transpose(to[0:R, i * P:(i + 1) * P], u_mask[:, 4 * half + i, :], ident[:, :])
                    last.then_inc(s_ut, 1)
                pe.wait_ge(s_w_lo, chunk(pr, W_T5) + 2)
                pe.wait_ge(s_u_lo, pr * 2 + 2)
                burst(2, pr, 0, range(BTILES), ffn_left(2), [wo(0), wo(1)], extra=wkv)
                pe.wait_ge(s_w_lo, chunk(pr, W_T7) + 2)
                burst(3, pr, 0, range(BTILES), ffn_left(3), [wq(0), wq(1)])

                pe.wait_ge(s_w_lo, chunk(pr, W_K0) + 2)
                project(ps_t0[:, :], wkv, 0).then_inc(s_kv, 1)
                project(ps_t1[:, :], wkv, 1).then_inc(s_kv, 1)
                pe.wait_ge(s_w_lo, chunk(pr, W_V0) + 2)
                pe.wait_ge(s_acc, burst_base(pr, 4))
                project(ps_b[:, :], wo(0), 0).then_inc(s_kv, 1)
                project(ps_c[:, :], wo(0), 1).then_inc(s_kv, 1)
                pe.wait_ge(s_w_lo, chunk(pr, W_Q0) + 2)
                project(ps_q[:, :], wq(0), 0).then_inc(s_q, 1)
                pe.wait_ge(s_kv_out, group(pr, 0) * 4 + 4)
                values()

            def values():
                for b, to in enumerate((ps_t0, ps_t1)):
                    for i in range(QT):
                        last = pe.transpose(to[:, i * P:(i + 1) * P],
                                            next_v[:, b * SEQ + i * P:b * SEQ + (i + 1) * P], ident[:, :])
                    last.then_inc(s_vt, 1)

            def transposes(pr, g, n, last_group):
                pe.wait_ge(s_probs, unit(pr, g, n) + 1)
                if n == 0:
                    pe.wait_ge(s_v_lo, (group(pr, g) + 1) * 2)
                for (to, _, _), tiles in zip(t_banks(last_group), (
                        [(0, i) for i in range(4)], [(1, 1), (1, 2), (1, 3), (3, 3)], [(2, 2), (2, 3)])):
                    if to is ps_o:
                        pe.wait_ge(s_at_lo, unit(pr, g, n) + 1)
                    if to is ps_kv and n == 4:
                        pe.wait_ge(s_acc, burst_base(pr, FFN_BURSTS, g) + (BTILES - 3))
                    for c, (j, i) in enumerate(tiles):
                        last = pe.transpose(to[:, c * P:(c + 1) * P],
                                            probs[:, OFF[i] + j * P:OFF[i] + (j + 1) * P], ident[:, :])
                    last.then_inc(s_pt, 1)

            def scores(pr, g, n):
                b = n % 2
                if n == 0:
                    pe.wait_ge(s_k_lo, group(pr, g) + 1)
                pe.wait_ge(s_q_lo, unit(pr, g, n) + 1)
                if n in (0, 5):
                    pe.wait_ge(s_acc, burst_base(pr, FFN_BURSTS + n // 5, g) - (2 if n == 0 else 0))
                for i in (3, 2, 0, 1):
                    keys = slice(b * SEQ, b * SEQ + (i + 1) * P)
                    last = product(score_bank[i], (q_hi[:, i * P:(i + 1) * P], q_lo[:, i * P:(i + 1) * P]),
                                   (k_hi[:, keys], k_lo[:, keys]), True, True)
                    if i != 0:
                        last.then_inc(s_scores, 1)

            def attend(pr, g, n):
                b = n % 2
                if n == 0:
                    pe.wait_ge(s_v_lo, (group(pr, g) + 1) * 2)
                pe.wait_ge(s_pt_lo, unit(pr, g, n) * 3 + 3)
                for j in (0, 1, 3, 2):
                    width = SEQ - j * P
                    tile = slice(b * SEQ + j * P, b * SEQ + (j + 1) * P)
                    last = product(ps_o[:, j * P:SEQ], (v_hi[:, tile], v_lo[:, tile]),
                                   (pt_hi[:, TOFF[j]:TOFF[j] + width], pt_lo[:, TOFF[j]:TOFF[j] + width]),
                                   j == 0, j == 2)
                last.then_inc(s_o, 1)

            def next_queries(pr, g, n, last_group):
                head = (n + 1) // 2
                if n % 2:
                    name = (None, C_Q1, C_Q2, C_Q3, C_Q0)[head]
                    k = group_chunk(name, last_group) + (g * PER_GROUP if last_group else 0)
                    pe.wait_ge(s_w_lo, chunk(pr, k, 0 if last_group else g) + 2)
                last = project(ps_q[:, :], wq(head % 2), (n + 1) % 2)
                last.then_inc(s_q, 1)

            def next_keys_values(pr, g, n):
                if n == 0:
                    pe.wait_ge(s_w_lo, chunk(pr, BEFORE - 1, g) + 2)
                    pe.wait_ge(s_acc, burst_base(pr, FFN_BURSTS, g))
                if n == 4:
                    pe.wait_ge(s_w_lo, chunk(pr, BEFORE + C_V, g) + 2)
                if n % 2 == 0:
                    pe.wait_ge(s_kv_out, (group(pr, g) + 1) * 4 + n // 2)
                last = project(ps_kv[:, :], wkv, (n // 2) % 2, range(4 * (n % 2), 4 * (n % 2) + 4))
                if n % 2:
                    last.then_inc(s_kv, 1)

            def heads_burst(pr, g, which, tiles, last_group):
                b, part = FFN_BURSTS + which, tiles[0] // (BTILES // 2)
                if tiles[0] == 0:
                    k = group_chunk((C_O1, C_O3)[which], last_group) + (g * PER_GROUP if last_group else 0)
                    pe.wait_ge(s_w_lo, chunk(pr, k, 0 if last_group else g) + 2)
                    pe.wait_ge(s_neg_max, unit(pr, g, 4 + 3 * which) * QT + 2)
                    if not (last_group and which == 1):
                        pe.wait_ge(s_q_lo, unit(pr, g, 6 + 3 * which))
                    if not last_group:
                        pe.wait_ge(s_kv_out, (group(pr, g) + 1) * 4 + 2 + 2 * which)
                pe.wait_ge(s_at_lo, unit(pr, g, 4 * which + 2 + part) + 2)
                burst(b, pr, g, tiles, ats, [wo(0), wo(1)])

            def one_group(pr, g, last_group):
                for n in range(UNITS):
                    if n:
                        transposes(pr, g, n - 1, last_group)
                    scores(pr, g, n)
                    if n < UNITS - 1 or not last_group:
                        if n in (0, 5):
                            pe.wait_ge(s_acc, burst_base(pr, FFN_BURSTS + (n > 0), g))
                        next_queries(pr, g, n, last_group)
                    if n:
                        attend(pr, g, n - 1)
                    if n == 4:
                        heads_burst(pr, g, 0, range(0, BTILES // 2), last_group)
                        heads_burst(pr, g, 0, range(BTILES // 2, BTILES), last_group)
                    if not last_group:
                        if n == 4:
                            pe.wait_ge(s_acc, burst_base(pr, FFN_BURSTS, g) + (BTILES - 3))
                        next_keys_values(pr, g, n)
                transposes(pr, g, UNITS - 1, last_group)
                heads_burst(pr, g, 1, range(0, 3), last_group)
                if last_group:
                    pe.wait_ge(s_pt_lo, unit(pr, g, UNITS) * 3)
                heads_burst(pr, g, 1, range(3, 5), last_group)
                attend(pr, g, UNITS - 1)
                heads_burst(pr, g, 1, range(5, BTILES // 2), last_group)
                if not last_group:
                    pe.wait_ge(s_kv_out, (group(pr, g) + 1) * 4 + 4)
                    values()
                heads_burst(pr, g, 1, range(BTILES // 2, BTILES), last_group)

            pe.sem_inc(s_burst, 1)
            pe.wait_ge(s_const, 64)
            with pe.Fori(0, PAIRS) as pr:
                before_groups(pr)
                with pe.Fori(0, KV_HEADS - 1) as g:
                    one_group(pr, g, False)
                one_group(pr, KV_HEADS - 1, True)

        def weight_of(k, last):
            return {C_Q1: wq(1), C_O0: wo(0), C_Q2: wq(0), C_O1: wo(1), C_Q3: wq(1), C_V: wkv,
                    C_O2: wo(0), C_Q0: wq(0), C_O3: wo(1), C_K: wkv}[k]

        SPLIT_IN = {0: [C_Q1], 1: [C_O0, C_Q2], 2: [C_O1], 3: [C_Q3], 4: [C_V], 5: [C_O2, C_Q0],
                    6: [C_O3], 7: [], None: [C_K]}

        def group_splits(n, last):
            return [k for k in SPLIT_IN[n] if not (last and k in (C_V, C_Q0, C_K))]

        @block.scalar
        def _(act):
            def high(to, source, signal):
                nc.scalar.activation(to, source, ACT.Copy).then_inc(signal, 1)

            def weights(pr, k, to, g=0, rows=P, cols=HIDDEN):
                slot = k % 2
                loaded = pr * (16 * ((CHUNKS + 1 - slot) // 2)) + g * (16 * PER_GROUP // 2) + 16 * (k // 2 + 1)
                act.wait_ge(s_loaded[slot], loaded)
                high(to[0][0:rows, 0:cols], stage[0:rows, slot, 0:cols], s_w_hi)

            def group_weights(pr, g, n, last_group):
                for k in group_splits(n, last_group):
                    if k in (C_Q1, C_Q2, C_Q3, C_Q0):
                        done = {C_Q1: 1, C_Q2: 2, C_Q3: 4, C_Q0: 6}[k]
                        act.wait_ge(s_q, unit(pr, g, 0) + done)
                    elif k in (C_O0, C_O1, C_O2, C_O3):
                        b = FFN_BURSTS + (k in (C_O2, C_O3))
                        act.wait_ge(s_burst, burst_base(pr, b, g) + 1)
                    else:
                        act.wait_ge(s_kv, (group(pr, g) + 1) * 4 + {C_V: 2, C_K: 4}[k])
                    if last_group:
                        weights(pr, group_chunk(k, True) + g * PER_GROUP, weight_of(k, True))
                    else:
                        weights(pr, group_chunk(k, False), weight_of(k, False), g)

            def transposed(pr, g, n, last_group):
                for i, (ps, at, width) in enumerate(t_banks(last_group)):
                    act.wait_ge(s_pt, unit(pr, g, n) * 3 + i + 1)
                    high(pt_hi[:, at:at + width], ps[:, 0:width], s_pt_hi)

            def exponentials(pr, g, n):
                for c, i in enumerate((3, 2, 0, 1)):
                    act.wait_ge(s_neg_max, unit(pr, g, n) * QT + c + 1)
                    tile = probs[:, OFF[i]:OFF[i] + (i + 1) * P]
                    nc.scalar.activation(tile, tile, ACT.Exp, bias=neg_max[:, i:i + 1], scale=-1.0,
                                         accum_out=row_sum[:, i:i + 1]).then_inc(s_exp, 1)

            def queries(pr, g, n):
                act.wait_ge(s_q, unit(pr, g, n) + 1)
                high(q_hi[:, :], ps_q[:, :], s_q_hi)

            def outputs(pr, g, n):
                act.wait_ge(s_o, unit(pr, g, n) + 1)
                high(at_hi[:, (n // 2) % 2, (n % 2) * SEQ:(n % 2 + 1) * SEQ], ps_o[:, :], s_at_hi)

            def keys(pr, gt):
                act.wait_ge(s_kv_out, gt * 4 + 2)
                high(k_hi[:, :], next_k[:, :], s_k_hi)

            def values(gt):
                for b, ps in enumerate((ps_t0, ps_t1)):
                    act.wait_ge(s_vt, gt * 2 + b + 1)
                    high(v_hi[:, b * SEQ:(b + 1) * SEQ], ps[:, :], s_v_hi)

            def root_of(pr, q):
                act.wait_ge(s_var, pr * (TT // 2) + q + 1)
                nc.scalar.activation(root[:, :], root[:, :], ACT.Sqrt).then_inc(s_std, 1)

            def one_group(pr, g, last_group):
                for n in range(UNITS):
                    if n:
                        transposed(pr, g, n - 1, last_group)
                    exponentials(pr, g, n)
                    group_weights(pr, g, n, last_group)
                    if n == UNITS - 1 and not last_group:
                        keys(pr, group(pr, g) + 1)
                    if n < UNITS - 1 or not last_group:
                        queries(pr, g, n + 1)
                    if n:
                        outputs(pr, g, n - 1)
                transposed(pr, g, UNITS - 1, last_group)
                group_weights(pr, g, None, last_group)
                outputs(pr, g, UNITS - 1)
                if not last_group:
                    values(group(pr, g) + 1)

            with act.Fori(0, PAIRS) as pr:
                for tt in range(TT):
                    act.wait_ge(s_acc_free, pr * TT + tt + 1)
                    act.dma_start(acc[:, tt, :], x[bass.ds(pr * PT + tt * P, P), :]).then_inc(s_x[tt], 16)
                act.wait_ge(s_burst, burst_base(pr, 0) + 1)
                root_of(pr, 0)
                weights(pr, W_AG, wkv, cols=HT * AG)
                weights(pr, W_T0, wo(0))
                weights(pr, W_T1, wo(1))
                for tt in range(TT):
                    if tt % 2 == 0 and tt // 2 + 1 < TT // 2:
                        root_of(pr, tt // 2 + 1)
                    for half in range(2):
                        act.wait_ge(s_xt, pr * (2 * TT) + 2 * tt + half + 1)
                        ps = ((ps_t0, ps_t1), (ps_b, ps_c))[tt % 2][half]
                        high(x_hi[:, 4 * half:4 * half + 4, tt * P:(tt + 1) * P],
                             ps[:, :].rearrange("p (h t) -> p h t", h=4), s_x_hi)
                    if tt == 2:
                        weights(pr, W_T2, wq(0))
                    if tt == 4:
                        weights(pr, W_T3, wq(1))
                act.wait_ge(s_ag, pr * 2 + 2)
                weights(pr, W_LORA, wkv, rows=LK)
                act.wait_ge(s_gate, pr + 1)
                nc.scalar.activation(gate_buf[:, 1], gate_buf[:, 1], ACT.Exp).then_inc(s_gate_exp, 1)
                act.wait_ge(s_burst, burst_base(pr, 1) + 1)
                weights(pr, W_T4, wo(0))
                weights(pr, W_T5, wo(1))
                for half, ps in enumerate((ps_t0, ps_t1)):
                    act.wait_ge(s_ut, pr * 2 + half + 1)
                    high(at_hi[0:R, 0, half * 512:(half + 1) * 512], ps[0:R, :], s_u_hi)
                act.wait_ge(s_burst, burst_base(pr, 2) + 1)
                weights(pr, W_T6, wq(0))
                weights(pr, W_T7, wq(1))
                act.wait_ge(s_burst, burst_base(pr, 3) + 1)
                weights(pr, W_K0, wkv)
                weights(pr, W_V0, wo(0))
                act.wait_ge(s_burst, burst_base(pr, 4) + 1)
                weights(pr, W_Q0, wq(0))
                act.wait_ge(s_kv, group(pr, 0) * 4 + 2)
                weights(pr, W_K1, wkv)
                keys(pr, group(pr, 0))
                queries(pr, 0, 0)
                values(group(pr, 0))
                with act.Fori(0, KV_HEADS - 1) as g:
                    one_group(pr, g, False)
                one_group(pr, KV_HEADS - 1, True)

        @block.vector
        def _(dve):
            links = [0]

            def link(pr, ins):
                links[0] += 1
                ins.then_inc(s_link, 1)
                dve.wait_ge(s_link, pr * LINKS + links[0])

            def low(to, source, high, signal):
                nc.vector.tensor_tensor(to, source, high.bitcast(F32), ALU.subtract).then_inc(signal, 1)

            def weights(pr, k, to, g=0, rows=P, cols=HIDDEN):
                dve.wait_ge(s_w_hi, chunk(pr, k, g) + 1)
                low(to[1][0:rows, 0:cols], stage[0:rows, k % 2, 0:cols], to[0][0:rows, 0:cols], s_w_lo)

            def group_weights(pr, g, n, last_group):
                for k in group_splits(n, last_group):
                    if last_group:
                        weights(pr, group_chunk(k, True) + g * PER_GROUP, weight_of(k, True))
                    else:
                        weights(pr, group_chunk(k, False), weight_of(k, False), g)

            def transposed(pr, g, n, last_group):
                for i, (ps, at, width) in enumerate(t_banks(last_group)):
                    dve.wait_ge(s_pt_hi, unit(pr, g, n) * 3 + i + 1)
                    low(pt_lo[:, at:at + width], ps[:, 0:width], pt_hi[:, at:at + width], s_pt_lo)

            def bias_of(head):
                nc.vector.tensor_scalar(head_bias[:, :], dist[:, :], slopes[:, bass.ds(head, 1)], None,
                                        ALU.mult).then_inc(s_bias, 1)

            def maxima(pr, g, n):
                if n % 2 == 0:
                    dve.wait_ge(s_bias, pr * HEADS + g * G + n // 2 + 1)
                for c, i in enumerate((3, 2, 0, 1)):
                    if i != 1:
                        dve.wait_ge(s_scores, unit(pr, g, n) * 3 + c + 1)
                        settled(dve)
                    nc.vector.tensor_tensor_reduce(
                        out=probs[:, OFF[i]:OFF[i] + (i + 1) * P], in0=score_bank[i],
                        in1=head_bias[:, SEQ - (i + 1) * P:SEQ], scale=-SCALE, scalar=3e38,
                        op0=ALU.add, op1=ALU.min, accum_out=neg_max[:, i:i + 1]).then_inc(s_neg_max, 1)

            def normalise(pr, g, n):
                dve.wait_ge(s_exp, unit(pr, g, n) * QT + QT)
                nc.vector.reciprocal(row_inv[:, :], row_sum[:, :]).then_inc(s_inv, 1)
                dve.wait_ge(s_inv, unit(pr, g, n) + 1)
                for i in range(QT):
                    tile = probs[:, OFF[i]:OFF[i] + (i + 1) * P]
                    last = nc.vector.tensor_scalar(tile, tile, row_inv[:, i:i + 1], None, ALU.mult)
                last.then_inc(s_probs, 1)

            def queries(pr, g, n):
                dve.wait_ge(s_q_hi, unit(pr, g, n) + 1)
                low(q_lo[:, :], ps_q[:, :], q_hi[:, :], s_q_lo)

            def outputs(pr, g, n):
                dve.wait_ge(s_at_hi, unit(pr, g, n) + 1)
                at = (slice(None), (n // 2) % 2, slice((n % 2) * SEQ, (n % 2 + 1) * SEQ))
                low(at_lo[at], ps_o[:, :], at_hi[at], s_at_lo)

            def copy_piece(gt, piece, ps):
                dve.wait_ge(s_kv, gt * 4 + piece + 1)
                to = (next_k, next_v)[piece // 2]
                nc.vector.tensor_copy(to[:, (piece % 2) * SEQ:(piece % 2 + 1) * SEQ], ps[:, :]).then_inc(s_kv_out, 1)

            def keys(gt):
                dve.wait_ge(s_k_hi, gt + 1)
                low(k_lo[:, :], next_k[:, :], k_hi[:, :], s_k_lo)

            def values(gt):
                for b, ps in enumerate((ps_t0, ps_t1)):
                    dve.wait_ge(s_v_hi, gt * 2 + b + 1)
                    low(v_lo[:, b * SEQ:(b + 1) * SEQ], ps[:, :], v_hi[:, b * SEQ:(b + 1) * SEQ], s_v_lo)

            def add(pr, b, tiles, g=0):
                for r in tiles:
                    dve.wait_ge(s_burst, burst_base(pr, b, g) + r + 2)
                    to = acc[:, r // HALVES, (r % HALVES) * 512:(r % HALVES + 1) * 512]
                    banks = ring(b)
                    nc.vector.tensor_tensor(to, banks[r % len(banks)][:, :], to, ALU.add).then_inc(s_acc, 1)

            def inverse_deviation(pr, q):
                for i in range(2):
                    dve.wait_ge(s_x[2 * q + i], (pr + 1) * 16)
                    for half in range(2):
                        last = nc.vector.bn_stats(stats[:, i, half, :], acc[:, 2 * q + i, half * 512:(half + 1) * 512])
                link(pr, last)
                settled(dve)
                mom = moments[:, q % 2]
                for i in range(2):
                    last = nc.vector.bn_aggr(mom[:, i, :], stats[:, i])
                link(pr, last)
                r = rstd[:, 2 * q:2 * q + 2]
                nc.vector.tensor_scalar(root[:, :], mom[:, :, 1], EPS, None, ALU.add).then_inc(s_var, 1)
                dve.wait_ge(s_std, pr * (TT // 2) + q + 1)
                link(pr, nc.vector.reciprocal(r, root[:, :]))
                link(pr, nc.vector.scalar_tensor_tensor(newton[:, :], mom[:, :, 1], EPS, r, ALU.add, ALU.mult))
                link(pr, nc.vector.tensor_tensor(newton[:, :], newton[:, :], r, ALU.mult))
                link(pr, nc.vector.tensor_scalar(newton[:, :], newton[:, :], -0.5, 1.5, ALU.mult, ALU.add))
                link(pr, nc.vector.tensor_tensor(r, r, newton[:, :], ALU.mult))

            def normalised(pr, tt):
                if tt >= 2:
                    dve.wait_ge(s_xt, pr * (2 * TT) + 2 * (tt - 1))
                nc.vector.tensor_scalar(normed[tt % 2], acc[:, tt, :], moments[:, (tt // 2) % 2, tt % 2, 0:1],
                                        rstd[:, tt:tt + 1], ALU.subtract, ALU.mult).then_inc(s_xn, 1)

            def gate_scores(pr):
                z, d = gate_buf[:, 0], gate_buf[:, 1]
                link(pr, nc.vector.tensor_tensor(z, ag_out[:, :, R:AG],
                                                 gbias[:, :].unsqueeze(1).to_broadcast([P, TT, E]), ALU.add))
                link(pr, nc.vector.tensor_reduce(gate_col[:, 0], z, AX.X, ALU.max))
                nc.vector.tensor_tensor(d, z, gate_col[:, 0].unsqueeze(2).to_broadcast([P, TT, E]),
                                        ALU.subtract).then_inc(s_gate, 1)

            def gate_masks(pr):
                p = gate_buf[:, 0]
                e, inv, top, rtop, weight, p01, p012 = gate_buf[:, 1], *(gate_col[:, i] for i in range(1, 7))
                total = gate_col[:, 0]
                dve.wait_ge(s_gate_exp, pr + 1)
                link(pr, nc.vector.tensor_reduce(total, e, AX.X, ALU.add))
                link(pr, nc.vector.reciprocal(inv, total))
                link(pr, nc.vector.tensor_tensor(p, e, inv.unsqueeze(2).to_broadcast([P, TT, E]), ALU.mult))
                nc.vector.tensor_tensor(p01, p[:, :, 0], p[:, :, 1], ALU.max)
                link(pr, nc.vector.tensor_reduce(top, p, AX.X, ALU.max))
                nc.vector.tensor_tensor(p012, p01, p[:, :, 2], ALU.max)
                link(pr, nc.vector.reciprocal(rtop, top))
                link(pr, nc.vector.tensor_tensor(weight, top, rtop, ALU.mult))
                chosen = [gate_col[:, 7 + i] for i in range(3)]
                for to, before in zip(chosen, (p[:, :, 0], p01, p012)):
                    last = nc.vector.tensor_tensor(to, before, top, ALU.is_lt)
                link(pr, last)
                for to in chosen:
                    last = nc.vector.tensor_tensor(to, to, weight, ALU.mult)
                link(pr, last)
                lows = (0,) + RANKS[:-1]
                for low_rank, rank, w in zip(lows, RANKS, [weight] + chosen):
                    last = nc.vector.tensor_tensor(
                        u_mask[:, :, low_rank:rank], ag_out[:, :, low_rank:rank],
                        w.unsqueeze(2).to_broadcast([P, TT, rank - low_rank]), ALU.mult)
                last.then_inc(s_u, 1)

            def one_group(pr, g, last_group):
                for n in range(UNITS):
                    if n:
                        transposed(pr, g, n - 1, last_group)
                    maxima(pr, g, n)
                    normalise(pr, g, n)
                    if n % 2 and (n < UNITS - 1 or not last_group):
                        bias_of(g * G + (n + 1) // 2)
                    group_weights(pr, g, n, last_group)
                    if n == UNITS - 1 and not last_group:
                        keys(group(pr, g) + 1)
                    if n < UNITS - 1 or not last_group:
                        queries(pr, g, n + 1)
                    if n:
                        outputs(pr, g, n - 1)
                    if n == 4:
                        add(pr, FFN_BURSTS, range(BTILES), g)
                    if n % 2 and not last_group:
                        copy_piece(group(pr, g) + 1, n // 2, ps_kv)
                transposed(pr, g, UNITS - 1, last_group)
                group_weights(pr, g, None, last_group)
                add(pr, FFN_BURSTS + 1, range(0, 5), g)
                outputs(pr, g, UNITS - 1)
                add(pr, FFN_BURSTS + 1, range(5, BTILES // 2), g)
                if not last_group:
                    values(group(pr, g) + 1)
                add(pr, FFN_BURSTS + 1, range(BTILES // 2, BTILES), g)

            dve.sem_inc(s_w_lo, 1)
            dve.sem_inc(s_at_lo, 1)
            dve.wait_ge(s_const, 64)
            with dve.Fori(0, PAIRS) as pr:
                inverse_deviation(pr, 0)
                normalised(pr, 0)
                weights(pr, W_AG, wkv, cols=HT * AG)
                weights(pr, W_T0, wo(0))
                weights(pr, W_T1, wo(1))
                for tt in range(TT + 1):
                    if tt < TT:
                        if tt % 2 == 0 and tt // 2 + 1 < TT // 2:
                            inverse_deviation(pr, tt // 2 + 1)
                        if tt + 1 < TT:
                            normalised(pr, tt + 1)
                        for half in range(2):
                            dve.wait_ge(s_x_hi, pr * (2 * TT) + 2 * tt + half + 1)
                            ps = ((ps_t0, ps_t1), (ps_b, ps_c))[tt % 2][half]
                            at = (slice(None), slice(4 * half, 4 * half + 4), slice(tt * P, (tt + 1) * P))
                            low(x_lo[at], ps[:, :].rearrange("p (h t) -> p h t", h=4), x_hi[at], s_x_lo)
                        if tt == 2:
                            weights(pr, W_T2, wq(0))
                        if tt == 4:
                            weights(pr, W_T3, wq(1))
                    if tt >= 1:
                        add(pr, 0, range(2 * (tt - 1), 2 * tt))
                nc.vector.memset(at_hi[R:LK, 0, :].bitcast(F32), 1.0)
                nc.vector.memset(at_lo[R:LK, 0, :].bitcast(F32), 0.0)
                for b, ps in enumerate((ps_a, ps_t0)):
                    dve.wait_ge(s_ag, pr * 2 + b + 1)
                    nc.vector.tensor_copy(ag_rows[:, b * SEQ:(b + 1) * SEQ], ps[0:AG, :]).then_inc(s_ag_row, 1)
                weights(pr, W_LORA, wkv, rows=LK)
                add(pr, 1, range(0, 4))
                for half, ps in enumerate((ps_a, ps_t1)):
                    dve.wait_ge(s_agt, pr * 2 + half + 1)
                    last = nc.vector.tensor_copy(ag_out[:, 4 * half:4 * half + 4, :],
                                                 ps[:, 0:4 * AG].rearrange("p (t a) -> p t a", a=AG))
                    last.then_inc(s_ag_out, 1)
                dve.wait_ge(s_ag_out, pr * 2 + 2)
                gate_scores(pr)
                add(pr, 1, range(4, 7))
                gate_masks(pr)
                add(pr, 1, range(7, 10))
                weights(pr, W_T4, wo(0))
                add(pr, 1, range(10, 12))
                weights(pr, W_T5, wo(1))
                add(pr, 1, range(12, BTILES))
                for half, ps in enumerate((ps_t0, ps_t1)):
                    dve.wait_ge(s_u_hi, pr * 2 + half + 1)
                    low(at_lo[0:R, 0, half * 512:(half + 1) * 512], ps[0:R, :],
                        at_hi[0:R, 0, half * 512:(half + 1) * 512], s_u_lo)
                weights(pr, W_T6, wq(0))
                add(pr, 2, range(0, 2))
                weights(pr, W_T7, wq(1))
                add(pr, 2, range(2, BTILES))
                weights(pr, W_K0, wkv)
                add(pr, 3, range(0, 2))
                weights(pr, W_V0, wo(0))
                add(pr, 3, range(2, BTILES))
                weights(pr, W_Q0, wq(0))
                copy_piece(group(pr, 0), 0, ps_t0)
                copy_piece(group(pr, 0), 1, ps_t1)
                weights(pr, W_K1, wkv)
                keys(group(pr, 0))
                copy_piece(group(pr, 0), 2, ps_b)
                copy_piece(group(pr, 0), 3, ps_c)
                bias_of(0)
                queries(pr, 0, 0)
                values(group(pr, 0))
                assert links[0] == LINKS, links
                with dve.Fori(0, KV_HEADS - 1) as g:
                    one_group(pr, g, False)
                one_group(pr, KV_HEADS - 1, True)


def constants():
    row = np.arange(P)[:, None]
    rel = row - (np.arange(SEQ)[None, :] - (SEQ - P))
    dist = np.where(rel >= 0, np.sqrt(np.maximum(rel, 0).astype(np.float32)), np.float32(MASKED))
    slopes = np.float32(2.0 ** (-8.0 / HEADS)) ** np.arange(1, HEADS + 1, dtype=np.float32)
    rows = np.broadcast_to(-slopes.astype(np.float64) / SCALE, (P, HEADS))
    return np.concatenate([dist, np.eye(P), rows], axis=1).astype(np.float32)


def kernel(L0_attn_hidden_states, L0_attn_w_qkv, L0_attn_w_o, L0_ffn_W, L0_ffn_b, L0_ffn_A, L0_ffn_B,
           L0_ffn_gate_w, L0_ffn_gate_b):
    import concourse.bacc as bacc
    from concourse.bass_utils import run_bass_kernel_spmd

    f = np.ascontiguousarray
    shape = L0_attn_hidden_states.shape
    w_qkv = np.asarray(L0_attn_w_qkv).reshape(HT, P, -1, P).transpose(2, 1, 0, 3).reshape(-1, HIDDEN)
    ag = np.concatenate([np.asarray(L0_ffn_A), np.asarray(L0_ffn_gate_w)]).T
    arrays = {
        "x": f(np.asarray(L0_attn_hidden_states).reshape(TOKENS, HIDDEN)),
        "w_qkv": f(w_qkv),
        "w_o": f(L0_attn_w_o),
        "w_ffn": f(np.asarray(L0_ffn_W).T),
        "w_ag": f(ag.reshape(HT, P, AG).transpose(1, 0, 2).reshape(P, HT * AG)),
        "w_lora": f(np.concatenate([np.asarray(L0_ffn_B).T, np.asarray(L0_ffn_b)[None, :]])),
        "gate_b": f(L0_ffn_gate_b),
        "consts": constants(),
    }
    nc = bacc.Bacc("TRN2", target_bir_lowering=False, num_devices=1)
    args = [nc.dram_tensor(n, a.shape, F32, kind="ExternalInput").ap() for n, a in arrays.items()]
    out = nc.dram_tensor("out", (TOKENS, HIDDEN), F32, kind="ExternalOutput").ap()
    block_program(nc, *args, out)
    result = run_bass_kernel_spmd(nc, [arrays], core_ids=[0])
    return result.results[0]["out"].reshape(shape)
```

```python
from contextlib import ExitStack

import numpy as np

import concourse.bass as bass
from concourse import mybir

ALU = mybir.AluOpType
ACT = mybir.ActivationFunctionType
AX = mybir.AxisListType
F32 = mybir.dt.float32
F32R = mybir.dt.float32r

P = 128
HIDDEN = 1024
HEADS = 32
KV_HEADS = 8
G = HEADS // KV_HEADS
D = 128
BATCH = 4
SEQ = 512
TOKENS = BATCH * SEQ
SCALE = float(D) ** -0.5
EPS = 1e-5
RANKS = (8, 16, 32, 64)
R = max(RANKS)
E = len(RANKS)

PAIRS = BATCH // 2
PT = TOKENS // PAIRS
TT = PT // P
HT = HIDDEN // P
QT = SEQ // P
UNITS = 2 * G
NP = QT * (QT + 1) // 2 * P
HALVES = HIDDEN // 512
BTILES = TT * HALVES
MASKED = 1e36
AG = R + E
LK = R + 1

OFF = [P * (i * (i + 1) // 2) for i in range(QT)]
TOFF = {0: 0, 1: 512, 3: 896, 2: 1024}

W_T0, W_T1, W_T2, W_T3, W_AG, W_T4, W_T5, W_T6, W_T7, W_LORA, W_K0, W_V0, W_Q0, W_K1 = range(14)
BEFORE = 14
C_Q1, C_O0, C_Q2, C_O1, C_Q3, C_V, C_O2, C_Q0, C_O3, C_K = range(10)
PER_GROUP = 10
L_Q1, L_O0, L_Q2, L_O1, L_Q3, L_O2, L_O3 = range(7)
CHUNKS = BEFORE + PER_GROUP * (KV_HEADS - 1) + 7

FFN_BURSTS = 3
BURSTS = FFN_BURSTS + 2 * KV_HEADS
NORM_GROUPS = ((0, 1), (2,), (3,), (4,), (5,), (6,), (7,))
LINKS = 6 * len(NORM_GROUPS) + 10


def block_program(nc, x, w_qkv, w_o, w_ffn, w_ag, w_lora, gate_b, consts, out):
    with ExitStack() as ctx:
        def sb(name, shape, dt=F32):
            return ctx.enter_context(nc.sbuf_tensor(name, shape, dt))

        def bank(name):
            return ctx.enter_context(nc.psum_tensor(name, [P, 512], F32))

        def sem(name):
            return ctx.enter_context(nc.semaphore(name))

        x_hi = sb("x_hi", [P, HT, PT], F32R)
        x_lo = sb("x_lo", [P, HT, PT], F32R)
        acc = sb("acc", [P, TT, HIDDEN])
        at_hi = sb("at_hi", [P, 2, PT], F32R)
        at_lo = sb("at_lo", [P, 2, PT], F32R)
        wo_hi = sb("wo_hi", [P, 2, HIDDEN], F32R)
        wo_lo = sb("wo_lo", [P, 2, HIDDEN], F32R)
        wq_hi = sb("wq_hi", [P, 2, HIDDEN], F32R)
        wq_lo = sb("wq_lo", [P, 2, HIDDEN], F32R)
        wkv_hi = sb("wkv_hi", [P, HIDDEN], F32R)
        wkv_lo = sb("wkv_lo", [P, HIDDEN], F32R)
        q_hi = sb("q_hi", [P, SEQ], F32R)
        q_lo = sb("q_lo", [P, SEQ], F32R)
        k_hi = sb("k_hi", [P, PT], F32R)
        k_lo = sb("k_lo", [P, PT], F32R)
        v_hi = sb("v_hi", [P, PT], F32R)
        v_lo = sb("v_lo", [P, PT], F32R)
        next_k = sb("next_k", [P, PT])
        next_v = sb("next_v", [P, PT])
        stage = sb("stage", [P, 2, HIDDEN])
        probs = sb("probs", [P, NP])
        pt_hi = sb("pt_hi", [P, NP], F32R)
        pt_lo = sb("pt_lo", [P, NP], F32R)
        dist = sb("dist", [P, SEQ])
        head_bias = sb("head_bias", [P, SEQ])
        ident = sb("ident", [P, P])
        slopes = sb("slopes", [P, HEADS])
        gbias = sb("gbias", [P, E])
        neg_max = sb("neg_max", [P, QT])
        row_sum = sb("row_sum", [P, QT])
        row_inv = sb("row_inv", [P, QT])

        ps_a, ps_b, ps_c = bank("ps_a"), bank("ps_b"), bank("ps_c")
        ps_t0, ps_t1 = bank("ps_t0"), bank("ps_t1")
        ps_o = bank("ps_o")
        ps_q, ps_kv = bank("ps_q"), bank("ps_kv")

        ag_rows = next_v[0:AG, :]
        ag_out = next_k[:, 0:TT * AG].rearrange("p (t a) -> p t a", a=AG)
        small = next_k[:, TT * AG:TT * AG + 80]
        stats = small[:, 0:24].rearrange("p (t h s) -> p t h s", t=2, h=2)
        moments = small[:, 24:40].rearrange("p (t m) -> p t m", m=2)
        rstd, root, newton, shift = (small[:, 40 + 8 * i:48 + 8 * i] for i in range(4))
        u_mask = probs[:, 0:TT * R].rearrange("p (t a) -> p t a", a=R)
        gate_buf = probs[:, TT * R:TT * (R + 2 * E)].rearrange("p (k t e) -> p k t e", k=2, e=E)
        gate_col = probs[:, TT * (R + 2 * E):TT * (R + 2 * E + 10)].rearrange("p (k t) -> p k t", t=TT)
        normed = [probs[:, 0:HIDDEN], next_v[:, :]]
        score_bank = {3: ps_c[:, :], 2: ps_b[:, 0:3 * P], 0: ps_a[:, 0:P], 1: ps_a[:, P:3 * P]}

        def t_banks(last_group):
            return [(ps_t0, 0, 512), (ps_t1, 512, 512), (ps_kv if last_group else ps_o, 1024, 256)]

        def ring(b):
            if b == 0:
                return [ps_q, ps_kv, ps_a, ps_o]
            if b < FFN_BURSTS:
                return [ps_q, ps_kv, ps_b, ps_c]
            return [ps_kv, ps_b, ps_c, ps_q] if b == FFN_BURSTS else [ps_b, ps_c, ps_q, ps_kv]

        s_ident = sem("s_ident")
        s_const = sem("s_const")
        s_x = [sem(f"s_x{i}") for i in range(TT)]
        s_loaded = [sem("s_loaded0"), sem("s_loaded1")]
        s_w_hi = sem("s_w_hi")
        s_w_lo = sem("s_w_lo")
        s_link = sem("s_link")
        s_var = sem("s_var")
        s_std = sem("s_std")
        s_rstd = sem("s_rstd")
        s_xn = sem("s_xn")
        s_xt = sem("s_xt")
        s_x_hi = sem("s_x_hi")
        s_x_lo = sem("s_x_lo")
        s_ag = sem("s_ag")
        s_ag_row = sem("s_ag_row")
        s_agt = sem("s_agt")
        s_ag_out = sem("s_ag_out")
        s_gate = sem("s_gate")
        s_gate_exp = sem("s_gate_exp")
        s_u = sem("s_u")
        s_ut = sem("s_ut")
        s_u_hi = sem("s_u_hi")
        s_u_lo = sem("s_u_lo")
        s_acc = sem("s_acc")
        s_burst = sem("s_burst")
        s_kv = sem("s_kv")
        s_kv_out = sem("s_kv_out")
        s_k_hi = sem("s_k_hi")
        s_k_lo = sem("s_k_lo")
        s_vt = sem("s_vt")
        s_v_hi = sem("s_v_hi")
        s_v_lo = sem("s_v_lo")
        s_q = sem("s_q")
        s_q_hi = sem("s_q_hi")
        s_q_lo = sem("s_q_lo")
        s_bias = sem("s_bias")
        s_scores = sem("s_scores")
        s_neg_max = sem("s_neg_max")
        s_exp = sem("s_exp")
        s_inv = sem("s_inv")
        s_probs = sem("s_probs")
        s_pt = sem("s_pt")
        s_pt_hi = sem("s_pt_hi")
        s_pt_lo = sem("s_pt_lo")
        s_o = sem("s_o")
        s_at_hi = sem("s_at_hi")
        s_at_lo = sem("s_at_lo")
        s_out = [sem(f"s_out{i}") for i in range(TT)]
        s_acc_free = sem("s_acc_free")
        s_settled = sem("s_settled")

        def unit(pr, g, n):
            return pr * (KV_HEADS * UNITS) + g * UNITS + n

        def group(pr, g):
            return pr * KV_HEADS + g

        def chunk(pr, k, g=0):
            return pr * CHUNKS + g * PER_GROUP + k

        def group_chunk(k, last):
            if not last:
                return BEFORE + k
            return BEFORE + {C_Q1: L_Q1, C_O0: L_O0, C_Q2: L_Q2, C_O1: L_O1, C_Q3: L_Q3,
                             C_O2: L_O2, C_O3: L_O3}[k]

        def burst_base(pr, b, g=0):
            return pr * (BURSTS * BTILES) + g * (2 * BTILES) + b * BTILES

        def wq(i):
            return wq_hi[:, i, :], wq_lo[:, i, :]

        def wo(i):
            return wo_hi[:, i, :], wo_lo[:, i, :]

        wkv = (wkv_hi[:, :], wkv_lo[:, :])

        block = ctx.enter_context(nc.Block())

        def settled(eng):
            eng.sem_inc(s_settled, 1)

        @block.sync
        def _(sp):
            sp.dma_start(ident[:, :], consts[:, SEQ:SEQ + P]).then_inc(s_ident, 16)
            sp.wait_ge(s_x[0], 16)

            def load(pr, k, source, g=0, rows=P, cols=HIDDEN):
                sp.wait_ge(s_w_lo, chunk(pr, max(k - 1, 0), g) + 1)
                sp.dma_start(stage[0:rows, k % 2, 0:cols], source).then_inc(s_loaded[k % 2], 16)

            def qkv(c):
                return w_qkv[bass.ds(c * P, P), :]

            def out_weights(h):
                return w_o[bass.ds(h * P, P), :]

            def group_loads(pr, g, last):
                order = [(C_Q1, qkv, g * G + 1), (C_O0, out_weights, g * G), (C_Q2, qkv, g * G + 2),
                         (C_O1, out_weights, g * G + 1), (C_Q3, qkv, g * G + 3),
                         (C_V, qkv, g + (HEADS + KV_HEADS + 1)), (C_O2, out_weights, g * G + 2),
                         (C_Q0, qkv, g * G + G), (C_O3, out_weights, g * G + 3),
                         (C_K, qkv, g + (HEADS + 2))]
                for k, source, index in order:
                    if last and k in (C_V, C_Q0, C_K):
                        continue
                    if last:
                        load(pr, group_chunk(k, last) + g * PER_GROUP, source(index))
                    else:
                        load(pr, group_chunk(k, last), source(index), g)

            with sp.Fori(0, PAIRS) as pr:
                load(pr, W_T0, w_ffn[0:P, :])
                load(pr, W_T1, w_ffn[P:2 * P, :])
                load(pr, W_T2, w_ffn[2 * P:3 * P, :])
                load(pr, W_T3, w_ffn[3 * P:4 * P, :])
                load(pr, W_AG, w_ag, cols=HT * AG)
                for k, t in ((W_T4, 4), (W_T5, 5), (W_T6, 6), (W_T7, 7)):
                    load(pr, k, w_ffn[t * P:(t + 1) * P, :])
                load(pr, W_LORA, w_lora, rows=LK)
                load(pr, W_K0, qkv(HEADS))
                load(pr, W_V0, qkv(HEADS + KV_HEADS))
                load(pr, W_Q0, qkv(0))
                load(pr, W_K1, qkv(HEADS + 1))
                with sp.Fori(0, KV_HEADS - 1) as g:
                    group_loads(pr, g, False)
                group_loads(pr, KV_HEADS - 1, True)

        @block.gpsimd
        def _(pool):
            pool.sem_inc(s_acc_free, TT)
            pool.wait_ge(s_x[1], 16)
            pool.dma_start(dist[:, :], consts[:, 0:SEQ]).then_inc(s_const, 16)
            pool.dma_start(slopes[:, :], consts[:, SEQ + P:SEQ + P + HEADS]).then_inc(s_const, 16)
            pool.dma_start(gbias[:, :], gate_b.partition_broadcast(P)).then_inc(s_const, 16)
            with pool.Fori(0, PAIRS) as pr:
                for tt in range(TT + 1):
                    if tt < TT:
                        pool.wait_ge(s_acc, burst_base(pr, BURSTS - 1) + (tt + 1) * HALVES)
                        pool.dma_start(out[bass.ds(pr * PT + tt * P, P), :], acc[:, tt, :]).then_inc(s_out[tt], 16)
                    if tt:
                        pool.wait_ge(s_out[tt - 1], pr * 16 + 16)
                        pool.sem_inc(s_acc_free, 1)

        @block.tensor
        def _(pe):
            def product(to, st, mv, start, stop):
                (st_hi, st_lo), (mv_hi, mv_lo) = st, mv
                pe.matmul(to, st_hi, mv_hi, start=start, stop=False)
                pe.matmul(to, st_hi, mv_lo, start=False, stop=False)
                return pe.matmul(to, st_lo, mv_hi, start=False, stop=stop)

            def xs(ht, a, b):
                return x_hi[:, ht, a:b], x_lo[:, ht, a:b]

            def cut(pair, a, b):
                return pair[0][:, a:b], pair[1][:, a:b]

            def project(to, w, b, tiles=range(HT)):
                for ht in tiles:
                    last = product(to, cut(w, ht * P, (ht + 1) * P), xs(ht, b * SEQ, (b + 1) * SEQ),
                                   ht == 0, ht == HT - 1)
                return last

            def burst(b, pr, g, tiles, left, weights, chunks=None, extra=None):
                banks = ring(b)
                for r in tiles:
                    tt, half = r // HALVES, r % HALVES
                    if r >= len(banks) or b == 2:
                        pe.wait_ge(s_acc, burst_base(pr, b, g) + (r - len(banks) + 1))
                    to = banks[r % len(banks)][:, :]
                    n = len(weights) + (extra is not None)
                    for i, w in enumerate(weights):
                        if chunks is not None and r == 0:
                            pe.wait_ge(s_w_lo, chunk(pr, chunks[i]) + 2)
                        last = product(to, left(i, tt * P, (tt + 1) * P), cut(w, half * 512, half * 512 + 512),
                                       i == 0, i == n - 1)
                    if extra is not None:
                        last = product(to, (at_hi[0:LK, 0, tt * P:(tt + 1) * P], at_lo[0:LK, 0, tt * P:(tt + 1) * P]),
                                       (extra[0][0:LK, half * 512:half * 512 + 512],
                                        extra[1][0:LK, half * 512:half * 512 + 512]), False, True)
                    last.then_inc(s_burst, 1)

            def ats(i, a, b):
                return at_hi[:, i, a:b], at_lo[:, i, a:b]

            def ffn_left(first):
                return lambda i, a, b: xs(first + i, a, b)

            def before_groups(pr):
                for tt in range(TT + 1):
                    if tt < TT:
                        pe.wait_ge(s_xn, pr * TT + tt + 1)
                        banks = ((ps_t0, ps_t1), (ps_b, ps_c))[tt % 2]
                        for half in range(2):
                            for i in range(4):
                                ht = 4 * half + i
                                last = pe.transpose(banks[half][:, i * P:(i + 1) * P],
                                                    normed[tt % 2][:, ht * P:(ht + 1) * P], ident[:, :])
                            last.then_inc(s_xt, 1)
                    if tt >= 1:
                        t = tt - 1
                        pe.wait_ge(s_x_lo, pr * (2 * TT) + 2 * (t + 1))
                        burst(0, pr, 0, range(2 * t, 2 * t + 2), ffn_left(0), [wq(0), wq(1), wo(0), wo(1)],
                              (W_T0, W_T1, W_T2, W_T3))

                pe.wait_ge(s_w_lo, chunk(pr, W_AG) + 2)
                for b, to in enumerate((ps_t0, ps_t1)):
                    for ht in range(HT):
                        last = product(to[0:AG, :], cut(wkv, ht * AG, (ht + 1) * AG),
                                       xs(ht, b * SEQ, (b + 1) * SEQ), ht == 0, ht == HT - 1)
                    last.then_inc(s_ag, 1)
                pe.wait_ge(s_acc, burst_base(pr, 1))
                second = (ffn_left(4), [wo(0), wo(1)], (W_T4, W_T5))
                burst(1, pr, 0, range(0, 2), *second)
                pe.wait_ge(s_ag_row, pr * 2 + 2)
                for half, to in enumerate((ps_a, ps_o)):
                    for i in range(4):
                        tt = 4 * half + i
                        last = pe.transpose(to[:, i * AG:(i + 1) * AG], ag_rows[:, tt * P:(tt + 1) * P],
                                            ident[0:AG, 0:AG])
                    last.then_inc(s_agt, 1)
                burst(1, pr, 0, range(2, 12), *second)

                pe.wait_ge(s_u, pr + 1)
                settled(pe)
                for half, to in enumerate((ps_t0, ps_t1)):
                    for i in range(4):
                        last = pe.transpose(to[0:R, i * P:(i + 1) * P], u_mask[:, 4 * half + i, :], ident[:, :])
                    last.then_inc(s_ut, 1)
                burst(1, pr, 0, range(12, BTILES), *second)
                pe.wait_ge(s_w_lo, chunk(pr, W_LORA) + 2)
                pe.wait_ge(s_u_lo, pr * 2 + 2)
                burst(2, pr, 0, range(BTILES), ffn_left(6), [wq(0), wq(1)], (W_T6, W_T7), extra=wkv)

                pe.wait_ge(s_w_lo, chunk(pr, W_K0) + 2)
                project(ps_t0[:, :], wo(0), 0).then_inc(s_kv, 1)
                project(ps_t1[:, :], wo(0), 1).then_inc(s_kv, 1)
                pe.wait_ge(s_w_lo, chunk(pr, W_V0) + 2)
                pe.wait_ge(s_acc, burst_base(pr, FFN_BURSTS))
                project(ps_b[:, :], wo(1), 0).then_inc(s_kv, 1)
                project(ps_c[:, :], wo(1), 1).then_inc(s_kv, 1)
                pe.wait_ge(s_w_lo, chunk(pr, W_Q0) + 2)
                project(ps_q[:, :], wq(0), 0).then_inc(s_q, 1)
                pe.wait_ge(s_kv_out, group(pr, 0) * 4 + 4)
                values()

            def values():
                for b, to in enumerate((ps_t0, ps_t1)):
                    for i in range(QT):
                        last = pe.transpose(to[:, i * P:(i + 1) * P],
                                            next_v[:, b * SEQ + i * P:b * SEQ + (i + 1) * P], ident[:, :])
                    last.then_inc(s_vt, 1)

            def transposes(pr, g, n, last_group):
                pe.wait_ge(s_probs, unit(pr, g, n) + 1)
                if n == 0:
                    pe.wait_ge(s_v_lo, (group(pr, g) + 1) * 2)
                for (to, _, _), tiles in zip(t_banks(last_group), (
                        [(0, i) for i in range(4)], [(1, 1), (1, 2), (1, 3), (3, 3)], [(2, 2), (2, 3)])):
                    if to is ps_o:
                        pe.wait_ge(s_at_lo, unit(pr, g, n) + 1)
                    if to is ps_kv and n == 4:
                        pe.wait_ge(s_acc, burst_base(pr, FFN_BURSTS, g) + (BTILES - 3))
                    for c, (j, i) in enumerate(tiles):
                        last = pe.transpose(to[:, c * P:(c + 1) * P],
                                            probs[:, OFF[i] + j * P:OFF[i] + (j + 1) * P], ident[:, :])
                    last.then_inc(s_pt, 1)

            def scores(pr, g, n):
                b = n % 2
                if n == 0:
                    pe.wait_ge(s_k_lo, group(pr, g) + 1)
                pe.wait_ge(s_q_lo, unit(pr, g, n) + 1)
                if n in (0, 5):
                    pe.wait_ge(s_acc, burst_base(pr, FFN_BURSTS + n // 5, g) - (2 if n == 0 else 0))
                for i in (3, 2, 0, 1):
                    keys = slice(b * SEQ, b * SEQ + (i + 1) * P)
                    last = product(score_bank[i], (q_hi[:, i * P:(i + 1) * P], q_lo[:, i * P:(i + 1) * P]),
                                   (k_hi[:, keys], k_lo[:, keys]), True, True)
                    if i != 0:
                        last.then_inc(s_scores, 1)

            def attend(pr, g, n):
                b = n % 2
                if n == 0:
                    pe.wait_ge(s_v_lo, (group(pr, g) + 1) * 2)
                pe.wait_ge(s_pt_lo, unit(pr, g, n) * 3 + 3)
                for j in (0, 1, 3, 2):
                    width = SEQ - j * P
                    tile = slice(b * SEQ + j * P, b * SEQ + (j + 1) * P)
                    last = product(ps_o[:, j * P:SEQ], (v_hi[:, tile], v_lo[:, tile]),
                                   (pt_hi[:, TOFF[j]:TOFF[j] + width], pt_lo[:, TOFF[j]:TOFF[j] + width]),
                                   j == 0, j == 2)
                last.then_inc(s_o, 1)

            def next_queries(pr, g, n, last_group):
                head = (n + 1) // 2
                if n % 2:
                    name = (None, C_Q1, C_Q2, C_Q3, C_Q0)[head]
                    k = group_chunk(name, last_group) + (g * PER_GROUP if last_group else 0)
                    pe.wait_ge(s_w_lo, chunk(pr, k, 0 if last_group else g) + 2)
                last = project(ps_q[:, :], wq(head % 2), (n + 1) % 2)
                last.then_inc(s_q, 1)

            def next_keys_values(pr, g, n):
                if n == 0:
                    pe.wait_ge(s_w_lo, chunk(pr, BEFORE - 1, g) + 2)
                    pe.wait_ge(s_acc, burst_base(pr, FFN_BURSTS, g))
                if n == 4:
                    pe.wait_ge(s_w_lo, chunk(pr, BEFORE + C_V, g) + 2)
                if n % 2 == 0:
                    pe.wait_ge(s_kv_out, (group(pr, g) + 1) * 4 + n // 2)
                last = project(ps_kv[:, :], wkv, (n // 2) % 2, range(4 * (n % 2), 4 * (n % 2) + 4))
                if n % 2:
                    last.then_inc(s_kv, 1)

            def heads_burst(pr, g, which, tiles, last_group):
                b, part = FFN_BURSTS + which, tiles[0] // (BTILES // 2)
                if tiles[0] == 0:
                    k = group_chunk((C_O1, C_O3)[which], last_group) + (g * PER_GROUP if last_group else 0)
                    pe.wait_ge(s_w_lo, chunk(pr, k, 0 if last_group else g) + 2)
                    pe.wait_ge(s_neg_max, unit(pr, g, 4 + 3 * which) * QT + 2)
                    if not (last_group and which == 1):
                        pe.wait_ge(s_q_lo, unit(pr, g, 6 + 3 * which))
                    if not last_group:
                        pe.wait_ge(s_kv_out, (group(pr, g) + 1) * 4 + 2 + 2 * which)
                pe.wait_ge(s_at_lo, unit(pr, g, 4 * which + 2 + part) + 2)
                burst(b, pr, g, tiles, ats, [wo(0), wo(1)])

            def one_group(pr, g, last_group):
                for n in range(UNITS):
                    if n:
                        transposes(pr, g, n - 1, last_group)
                    scores(pr, g, n)
                    if n < UNITS - 1 or not last_group:
                        if n in (0, 5):
                            pe.wait_ge(s_acc, burst_base(pr, FFN_BURSTS + (n > 0), g))
                        next_queries(pr, g, n, last_group)
                    if n:
                        attend(pr, g, n - 1)
                    if n == 4:
                        heads_burst(pr, g, 0, range(0, BTILES // 2), last_group)
                        heads_burst(pr, g, 0, range(BTILES // 2, BTILES), last_group)
                    if not last_group:
                        if n == 4:
                            pe.wait_ge(s_acc, burst_base(pr, FFN_BURSTS, g) + (BTILES - 3))
                        next_keys_values(pr, g, n)
                transposes(pr, g, UNITS - 1, last_group)
                heads_burst(pr, g, 1, range(0, 3), last_group)
                if last_group:
                    pe.wait_ge(s_pt_lo, unit(pr, g, UNITS) * 3)
                heads_burst(pr, g, 1, range(3, 5), last_group)
                attend(pr, g, UNITS - 1)
                heads_burst(pr, g, 1, range(5, BTILES // 2), last_group)
                if not last_group:
                    pe.wait_ge(s_kv_out, (group(pr, g) + 1) * 4 + 4)
                    values()
                heads_burst(pr, g, 1, range(BTILES // 2, BTILES), last_group)

            pe.sem_inc(s_burst, 1)
            pe.wait_ge(s_ident, 16)
            with pe.Fori(0, PAIRS) as pr:
                before_groups(pr)
                with pe.Fori(0, KV_HEADS - 1) as g:
                    one_group(pr, g, False)
                one_group(pr, KV_HEADS - 1, True)

        def weight_of(k, last):
            return {C_Q1: wq(1), C_O0: wo(0), C_Q2: wq(0), C_O1: wo(1), C_Q3: wq(1), C_V: wkv,
                    C_O2: wo(0), C_Q0: wq(0), C_O3: wo(1), C_K: wkv}[k]

        SPLIT_IN = {0: [C_Q1], 1: [C_O0, C_Q2], 2: [C_O1], 3: [C_Q3], 4: [C_V], 5: [C_O2, C_Q0],
                    6: [C_O3], 7: [], None: [C_K]}

        def group_splits(n, last):
            return [k for k in SPLIT_IN[n] if not (last and k in (C_V, C_Q0, C_K))]

        @block.scalar
        def _(act):
            def high(to, source, signal):
                nc.scalar.activation(to, source, ACT.Copy).then_inc(signal, 1)

            def weights(pr, k, to, g=0, rows=P, cols=HIDDEN):
                slot = k % 2
                loaded = pr * (16 * ((CHUNKS + 1 - slot) // 2)) + g * (16 * PER_GROUP // 2) + 16 * (k // 2 + 1)
                act.wait_ge(s_loaded[slot], loaded)
                high(to[0][0:rows, 0:cols], stage[0:rows, slot, 0:cols], s_w_hi)

            def group_weights(pr, g, n, last_group):
                for k in group_splits(n, last_group):
                    if k in (C_Q1, C_Q2, C_Q3, C_Q0):
                        done = {C_Q1: 1, C_Q2: 2, C_Q3: 4, C_Q0: 6}[k]
                        act.wait_ge(s_q, unit(pr, g, 0) + done)
                    elif k in (C_O0, C_O1, C_O2, C_O3):
                        b = FFN_BURSTS + (k in (C_O2, C_O3))
                        act.wait_ge(s_burst, burst_base(pr, b, g) + 1)
                    else:
                        act.wait_ge(s_kv, (group(pr, g) + 1) * 4 + {C_V: 2, C_K: 4}[k])
                    if last_group:
                        weights(pr, group_chunk(k, True) + g * PER_GROUP, weight_of(k, True))
                    else:
                        weights(pr, group_chunk(k, False), weight_of(k, False), g)

            def transposed(pr, g, n, last_group):
                for i, (ps, at, width) in enumerate(t_banks(last_group)):
                    act.wait_ge(s_pt, unit(pr, g, n) * 3 + i + 1)
                    high(pt_hi[:, at:at + width], ps[:, 0:width], s_pt_hi)

            def exponentials(pr, g, n):
                for c, i in enumerate((3, 2, 0, 1)):
                    act.wait_ge(s_neg_max, unit(pr, g, n) * QT + c + 1)
                    tile = probs[:, OFF[i]:OFF[i] + (i + 1) * P]
                    nc.scalar.activation(tile, tile, ACT.Exp, bias=neg_max[:, i:i + 1], scale=-1.0,
                                         accum_out=row_sum[:, i:i + 1]).then_inc(s_exp, 1)

            def queries(pr, g, n):
                act.wait_ge(s_q, unit(pr, g, n) + 1)
                high(q_hi[:, :], ps_q[:, :], s_q_hi)

            def outputs(pr, g, n):
                act.wait_ge(s_o, unit(pr, g, n) + 1)
                high(at_hi[:, (n // 2) % 2, (n % 2) * SEQ:(n % 2 + 1) * SEQ], ps_o[:, :], s_at_hi)

            def keys(gt):
                act.wait_ge(s_kv_out, gt * 4 + 2)
                high(k_hi[:, :], next_k[:, :], s_k_hi)

            def values(gt):
                for b, ps in enumerate((ps_t0, ps_t1)):
                    act.wait_ge(s_vt, gt * 2 + b + 1)
                    high(v_hi[:, b * SEQ:(b + 1) * SEQ], ps[:, :], s_v_hi)

            def load_tokens(pr, tiles):
                for tt in tiles:
                    act.wait_ge(s_acc_free, pr * TT + tt + 1)
                    act.dma_start(acc[:, tt, :], x[bass.ds(pr * PT + tt * P, P), :]).then_inc(s_x[tt], 16)

            def root_of(pr, q):
                at = slice(NORM_GROUPS[q][0], NORM_GROUPS[q][-1] + 1)
                act.wait_ge(s_var, pr * len(NORM_GROUPS) + q + 1)
                nc.scalar.activation(root[:, at], root[:, at], ACT.Sqrt).then_inc(s_std, 1)

            def normalised(pr, tt):
                q = [tt in tiles for tiles in NORM_GROUPS].index(True)
                act.wait_ge(s_rstd, pr * len(NORM_GROUPS) + q + 1)
                if tt >= 2:
                    act.wait_ge(s_xt, pr * (2 * TT) + 2 * (tt - 1))
                nc.scalar.activation(normed[tt % 2], acc[:, tt, :], ACT.Identity, bias=shift[:, tt:tt + 1],
                                     scale=rstd[:, tt:tt + 1]).then_inc(s_xn, 1)

            def one_group(pr, g, last_group):
                for n in range(UNITS):
                    if n:
                        transposed(pr, g, n - 1, last_group)
                    exponentials(pr, g, n)
                    group_weights(pr, g, n, last_group)
                    if n == UNITS - 1 and not last_group:
                        keys(group(pr, g) + 1)
                    if n < UNITS - 1 or not last_group:
                        queries(pr, g, n + 1)
                    if n:
                        outputs(pr, g, n - 1)
                transposed(pr, g, UNITS - 1, last_group)
                group_weights(pr, g, None, last_group)
                outputs(pr, g, UNITS - 1)
                if not last_group:
                    values(group(pr, g) + 1)

            with act.Fori(0, PAIRS) as pr:
                load_tokens(pr, range(0, 2))
                root_of(pr, 0)
                normalised(pr, 0)
                act.wait_ge(s_burst, pr * (burst_base(0, BURSTS - 1) + 1) + 1)
                weights(pr, W_T0, wq(0))
                normalised(pr, 1)
                load_tokens(pr, range(2, 4))
                weights(pr, W_T1, wq(1))
                act.wait_ge(s_burst, burst_base(pr, 0) + 1)
                for tt in range(TT):
                    if 1 <= tt < TT - 1:
                        root_of(pr, tt)
                    for half in range(2):
                        act.wait_ge(s_xt, pr * (2 * TT) + 2 * tt + half + 1)
                        ps = ((ps_t0, ps_t1), (ps_b, ps_c))[tt % 2][half]
                        high(x_hi[:, 4 * half:4 * half + 4, tt * P:(tt + 1) * P],
                             ps[:, :].rearrange("p (h t) -> p h t", h=4), s_x_hi)
                    if tt == 0:
                        weights(pr, W_T2, wo(0))
                        weights(pr, W_T3, wo(1))
                    elif tt < TT - 1:
                        normalised(pr, tt + 1)
                    if tt < 2:
                        load_tokens(pr, range(2 * tt + 4, 2 * tt + 6))
                    if tt == 5:
                        weights(pr, W_AG, wkv, cols=HT * AG)
                act.wait_ge(s_burst, burst_base(pr, 1) + 1)
                weights(pr, W_T4, wo(0))
                weights(pr, W_T5, wo(1))
                weights(pr, W_T6, wq(0))
                weights(pr, W_T7, wq(1))
                act.wait_ge(s_ag, pr * 2 + 2)
                weights(pr, W_LORA, wkv, rows=LK)
                act.wait_ge(s_gate, pr + 1)
                nc.scalar.activation(gate_buf[:, 1], gate_buf[:, 1], ACT.Exp).then_inc(s_gate_exp, 1)
                for half, ps in enumerate((ps_t0, ps_t1)):
                    act.wait_ge(s_ut, pr * 2 + half + 1)
                    high(at_hi[0:R, 0, half * 512:(half + 1) * 512], ps[0:R, :], s_u_hi)
                act.wait_ge(s_burst, burst_base(pr, 2) + 1)
                weights(pr, W_K0, wo(0))
                weights(pr, W_V0, wo(1))
                act.wait_ge(s_burst, burst_base(pr, 3) + 1)
                weights(pr, W_Q0, wq(0))
                weights(pr, W_K1, wkv)
                act.wait_ge(s_kv, group(pr, 0) * 4 + 2)
                keys(group(pr, 0))
                queries(pr, 0, 0)
                values(group(pr, 0))
                with act.Fori(0, KV_HEADS - 1) as g:
                    one_group(pr, g, False)
                one_group(pr, KV_HEADS - 1, True)

        @block.vector
        def _(dve):
            links = [0]

            def link(pr, ins):
                links[0] += 1
                ins.then_inc(s_link, 1)
                dve.wait_ge(s_link, pr * LINKS + links[0])

            def low(to, source, high, signal):
                nc.vector.tensor_tensor(to, source, high.bitcast(F32), ALU.subtract).then_inc(signal, 1)

            def weights(pr, k, to, g=0, rows=P, cols=HIDDEN):
                dve.wait_ge(s_w_hi, chunk(pr, k, g) + 1)
                low(to[1][0:rows, 0:cols], stage[0:rows, k % 2, 0:cols], to[0][0:rows, 0:cols], s_w_lo)

            def group_weights(pr, g, n, last_group):
                for k in group_splits(n, last_group):
                    if last_group:
                        weights(pr, group_chunk(k, True) + g * PER_GROUP, weight_of(k, True))
                    else:
                        weights(pr, group_chunk(k, False), weight_of(k, False), g)

            def transposed(pr, g, n, last_group):
                for i, (ps, at, width) in enumerate(t_banks(last_group)):
                    dve.wait_ge(s_pt_hi, unit(pr, g, n) * 3 + i + 1)
                    low(pt_lo[:, at:at + width], ps[:, 0:width], pt_hi[:, at:at + width], s_pt_lo)

            def bias_of(head):
                nc.vector.tensor_scalar(head_bias[:, :], dist[:, :], slopes[:, bass.ds(head, 1)], None,
                                        ALU.mult).then_inc(s_bias, 1)

            def maxima(pr, g, n):
                if n % 2 == 0:
                    dve.wait_ge(s_bias, pr * HEADS + g * G + n // 2 + 1)
                for c, i in enumerate((3, 2, 0, 1)):
                    if i != 1:
                        dve.wait_ge(s_scores, unit(pr, g, n) * 3 + c + 1)
                        settled(dve)
                    nc.vector.tensor_tensor_reduce(
                        out=probs[:, OFF[i]:OFF[i] + (i + 1) * P], in0=score_bank[i],
                        in1=head_bias[:, SEQ - (i + 1) * P:SEQ], scale=-SCALE, scalar=3e38,
                        op0=ALU.add, op1=ALU.min, accum_out=neg_max[:, i:i + 1]).then_inc(s_neg_max, 1)

            def normalise(pr, g, n):
                dve.wait_ge(s_exp, unit(pr, g, n) * QT + QT)
                nc.vector.reciprocal(row_inv[:, :], row_sum[:, :]).then_inc(s_inv, 1)
                dve.wait_ge(s_inv, unit(pr, g, n) + 1)
                for i in range(QT):
                    tile = probs[:, OFF[i]:OFF[i] + (i + 1) * P]
                    last = nc.vector.tensor_scalar(tile, tile, row_inv[:, i:i + 1], None, ALU.mult)
                last.then_inc(s_probs, 1)

            def queries(pr, g, n):
                dve.wait_ge(s_q_hi, unit(pr, g, n) + 1)
                low(q_lo[:, :], ps_q[:, :], q_hi[:, :], s_q_lo)

            def outputs(pr, g, n):
                dve.wait_ge(s_at_hi, unit(pr, g, n) + 1)
                at = (slice(None), (n // 2) % 2, slice((n % 2) * SEQ, (n % 2 + 1) * SEQ))
                low(at_lo[at], ps_o[:, :], at_hi[at], s_at_lo)

            def copy_piece(gt, piece, ps):
                dve.wait_ge(s_kv, gt * 4 + piece + 1)
                to = (next_k, next_v)[piece // 2]
                nc.vector.tensor_copy(to[:, (piece % 2) * SEQ:(piece % 2 + 1) * SEQ], ps[:, :]).then_inc(s_kv_out, 1)

            def keys(gt):
                dve.wait_ge(s_k_hi, gt + 1)
                low(k_lo[:, :], next_k[:, :], k_hi[:, :], s_k_lo)

            def values(gt):
                for b, ps in enumerate((ps_t0, ps_t1)):
                    dve.wait_ge(s_v_hi, gt * 2 + b + 1)
                    low(v_lo[:, b * SEQ:(b + 1) * SEQ], ps[:, :], v_hi[:, b * SEQ:(b + 1) * SEQ], s_v_lo)

            def add(pr, b, tiles, g=0):
                for r in tiles:
                    dve.wait_ge(s_burst, burst_base(pr, b, g) + r + 2)
                    to = acc[:, r // HALVES, (r % HALVES) * 512:(r % HALVES + 1) * 512]
                    banks = ring(b)
                    nc.vector.tensor_tensor(to, banks[r % len(banks)][:, :], to, ALU.add).then_inc(s_acc, 1)

            def inverse_deviation(pr, q):
                first, n = NORM_GROUPS[q][0], len(NORM_GROUPS[q])
                for i in range(n):
                    dve.wait_ge(s_x[first + i], (pr + 1) * 16)
                    for half in range(2):
                        last = nc.vector.bn_stats(stats[:, i, half, :], acc[:, first + i, half * 512:(half + 1) * 512])
                link(pr, last)
                settled(dve)
                for i in range(n):
                    last = nc.vector.bn_aggr(moments[:, first + i, :], stats[:, i])
                link(pr, last)
                at = slice(first, first + n)
                mean, variance = moments[:, at, 0], moments[:, at, 1]
                nc.vector.tensor_scalar(root[:, at], variance, EPS, None, ALU.add).then_inc(s_var, 1)
                dve.wait_ge(s_std, pr * len(NORM_GROUPS) + q + 1)
                link(pr, nc.vector.reciprocal(rstd[:, at], root[:, at]))
                link(pr, nc.vector.scalar_tensor_tensor(newton[:, at], variance, EPS, rstd[:, at], ALU.add, ALU.mult))
                link(pr, nc.vector.scalar_tensor_tensor(newton[:, at], newton[:, at], -0.5, rstd[:, at], ALU.mult, ALU.mult))
                link(pr, nc.vector.scalar_tensor_tensor(rstd[:, at], newton[:, at], 1.5, rstd[:, at], ALU.add, ALU.mult))
                nc.vector.scalar_tensor_tensor(shift[:, at], mean, -1.0, rstd[:, at], ALU.mult,
                                               ALU.mult).then_inc(s_rstd, 1)

            def gate_scores(pr):
                z, d = gate_buf[:, 0], gate_buf[:, 1]
                link(pr, nc.vector.tensor_tensor(z, ag_out[:, :, R:AG],
                                                 gbias[:, :].unsqueeze(1).to_broadcast([P, TT, E]), ALU.add))
                link(pr, nc.vector.tensor_reduce(gate_col[:, 0], z, AX.X, ALU.max))
                nc.vector.tensor_tensor(d, z, gate_col[:, 0].unsqueeze(2).to_broadcast([P, TT, E]),
                                        ALU.subtract).then_inc(s_gate, 1)

            def gate_weights(pr):
                p = gate_buf[:, 0]
                e, total, inv, top, rtop, weight, p01, p012 = gate_buf[:, 1], *(gate_col[:, i] for i in range(7))
                dve.wait_ge(s_gate_exp, pr + 1)
                link(pr, nc.vector.tensor_reduce(total, e, AX.X, ALU.add))
                link(pr, nc.vector.reciprocal(inv, total))
                link(pr, nc.vector.tensor_tensor(p, e, inv.unsqueeze(2).to_broadcast([P, TT, E]), ALU.mult))
                nc.vector.tensor_tensor(p01, p[:, :, 0], p[:, :, 1], ALU.max)
                link(pr, nc.vector.tensor_reduce(top, p, AX.X, ALU.max))
                nc.vector.tensor_tensor(p012, p01, p[:, :, 2], ALU.max)
                link(pr, nc.vector.reciprocal(rtop, top))

            def gate_masks(pr):
                top, rtop, weight, p01, p012, *chosen = (gate_col[:, i] for i in range(2, 10))
                link(pr, nc.vector.tensor_tensor(weight, top, rtop, ALU.mult))
                for to, before in zip(chosen, (gate_buf[:, 0, :, 0], p01, p012)):
                    last = nc.vector.tensor_tensor(to, before, top, ALU.is_lt)
                link(pr, last)
                for to in chosen:
                    last = nc.vector.tensor_tensor(to, to, weight, ALU.mult)
                link(pr, last)
                lows = (0,) + RANKS[:-1]
                for low_rank, rank, w in zip(lows, RANKS, [weight] + chosen):
                    last = nc.vector.tensor_tensor(
                        u_mask[:, :, low_rank:rank], ag_out[:, :, low_rank:rank],
                        w.unsqueeze(2).to_broadcast([P, TT, rank - low_rank]), ALU.mult)
                last.then_inc(s_u, 1)

            def one_group(pr, g, last_group):
                for n in range(UNITS):
                    if n:
                        transposed(pr, g, n - 1, last_group)
                    maxima(pr, g, n)
                    normalise(pr, g, n)
                    if n % 2 and (n < UNITS - 1 or not last_group):
                        bias_of(g * G + (n + 1) // 2)
                    group_weights(pr, g, n, last_group)
                    if n == UNITS - 1 and not last_group:
                        keys(group(pr, g) + 1)
                    if n < UNITS - 1 or not last_group:
                        queries(pr, g, n + 1)
                    if n:
                        outputs(pr, g, n - 1)
                    if n == 4:
                        add(pr, FFN_BURSTS, range(BTILES), g)
                    if n % 2 and not last_group:
                        copy_piece(group(pr, g) + 1, n // 2, ps_kv)
                transposed(pr, g, UNITS - 1, last_group)
                group_weights(pr, g, None, last_group)
                add(pr, FFN_BURSTS + 1, range(0, 5), g)
                outputs(pr, g, UNITS - 1)
                add(pr, FFN_BURSTS + 1, range(5, BTILES // 2), g)
                if not last_group:
                    values(group(pr, g) + 1)
                add(pr, FFN_BURSTS + 1, range(BTILES // 2, BTILES), g)

            dve.sem_inc(s_w_lo, 1)
            dve.sem_inc(s_at_lo, 1)
            with dve.Fori(0, PAIRS) as pr:
                inverse_deviation(pr, 0)
                weights(pr, W_T0, wq(0))
                weights(pr, W_T1, wq(1))
                for tt in range(TT + 1):
                    if 1 <= tt < TT - 1:
                        inverse_deviation(pr, tt)
                    if tt < TT:
                        for half in range(2):
                            dve.wait_ge(s_x_hi, pr * (2 * TT) + 2 * tt + half + 1)
                            ps = ((ps_t0, ps_t1), (ps_b, ps_c))[tt % 2][half]
                            at = (slice(None), slice(4 * half, 4 * half + 4), slice(tt * P, (tt + 1) * P))
                            low(x_lo[at], ps[:, :].rearrange("p (h t) -> p h t", h=4), x_hi[at], s_x_lo)
                        if tt == 0:
                            weights(pr, W_T2, wo(0))
                            weights(pr, W_T3, wo(1))
                        if tt == 5:
                            weights(pr, W_AG, wkv, cols=HT * AG)
                    if tt >= 1:
                        add(pr, 0, range(2 * (tt - 1), 2 * tt))
                weights(pr, W_T4, wo(0))
                weights(pr, W_T5, wo(1))
                nc.vector.memset(at_hi[R:LK, 0, :].bitcast(F32), 1.0)
                nc.vector.memset(at_lo[R:LK, 0, :].bitcast(F32), 0.0)
                weights(pr, W_T6, wq(0))
                weights(pr, W_T7, wq(1))
                for b, ps in enumerate((ps_t0, ps_t1)):
                    dve.wait_ge(s_ag, pr * 2 + b + 1)
                    nc.vector.tensor_copy(ag_rows[:, b * SEQ:(b + 1) * SEQ], ps[0:AG, :]).then_inc(s_ag_row, 1)
                weights(pr, W_LORA, wkv, rows=LK)
                add(pr, 1, range(0, 2))
                for half, ps in enumerate((ps_a, ps_o)):
                    dve.wait_ge(s_agt, pr * 2 + half + 1)
                    last = nc.vector.tensor_copy(ag_out[:, 4 * half:4 * half + 4, :],
                                                 ps[:, 0:4 * AG].rearrange("p (t a) -> p t a", a=AG))
                    last.then_inc(s_ag_out, 1)
                dve.wait_ge(s_const, 48)
                dve.wait_ge(s_ag_out, pr * 2 + 2)
                gate_scores(pr)
                add(pr, 1, range(2, 5))
                gate_weights(pr)
                add(pr, 1, range(5, 7))
                gate_masks(pr)
                add(pr, 1, range(7, 12))
                for half, ps in enumerate((ps_t0, ps_t1)):
                    dve.wait_ge(s_u_hi, pr * 2 + half + 1)
                    low(at_lo[0:R, 0, half * 512:(half + 1) * 512], ps[0:R, :],
                        at_hi[0:R, 0, half * 512:(half + 1) * 512], s_u_lo)
                add(pr, 1, range(12, BTILES))
                add(pr, 2, range(0, 2))
                weights(pr, W_K0, wo(0))
                add(pr, 2, range(2, 4))
                weights(pr, W_V0, wo(1))
                add(pr, 2, range(4, BTILES))
                weights(pr, W_Q0, wq(0))
                weights(pr, W_K1, wkv)
                copy_piece(group(pr, 0), 0, ps_t0)
                copy_piece(group(pr, 0), 1, ps_t1)
                keys(group(pr, 0))
                copy_piece(group(pr, 0), 2, ps_b)
                copy_piece(group(pr, 0), 3, ps_c)
                bias_of(0)
                queries(pr, 0, 0)
                values(group(pr, 0))
                assert links[0] == LINKS, links
                with dve.Fori(0, KV_HEADS - 1) as g:
                    one_group(pr, g, False)
                one_group(pr, KV_HEADS - 1, True)


def constants():
    row = np.arange(P)[:, None]
    rel = row - (np.arange(SEQ)[None, :] - (SEQ - P))
    dist = np.where(rel >= 0, np.sqrt(np.maximum(rel, 0).astype(np.float32)), np.float32(MASKED))
    slopes = np.float32(2.0 ** (-8.0 / HEADS)) ** np.arange(1, HEADS + 1, dtype=np.float32)
    rows = np.broadcast_to(-slopes.astype(np.float64) / SCALE, (P, HEADS))
    return np.concatenate([dist, np.eye(P), rows], axis=1).astype(np.float32)


def kernel(L0_attn_hidden_states, L0_attn_w_qkv, L0_attn_w_o, L0_ffn_W, L0_ffn_b, L0_ffn_A, L0_ffn_B,
           L0_ffn_gate_w, L0_ffn_gate_b):
    import concourse.bacc as bacc
    from concourse.bass_utils import run_bass_kernel_spmd

    f = np.ascontiguousarray
    shape = L0_attn_hidden_states.shape
    w_qkv = np.asarray(L0_attn_w_qkv).reshape(HT, P, -1, P).transpose(2, 1, 0, 3).reshape(-1, HIDDEN)
    ag = np.concatenate([np.asarray(L0_ffn_A), np.asarray(L0_ffn_gate_w)]).T
    arrays = {
        "x": f(np.asarray(L0_attn_hidden_states).reshape(TOKENS, HIDDEN)),
        "w_qkv": f(w_qkv),
        "w_o": f(L0_attn_w_o),
        "w_ffn": f(np.asarray(L0_ffn_W).T),
        "w_ag": f(ag.reshape(HT, P, AG).transpose(1, 0, 2).reshape(P, HT * AG)),
        "w_lora": f(np.concatenate([np.asarray(L0_ffn_B).T, np.asarray(L0_ffn_b)[None, :]])),
        "gate_b": f(L0_ffn_gate_b),
        "consts": constants(),
    }
    nc = bacc.Bacc("TRN2", target_bir_lowering=False, num_devices=1)
    args = [nc.dram_tensor(n, a.shape, F32, kind="ExternalInput").ap() for n, a in arrays.items()]
    out = nc.dram_tensor("out", (TOKENS, HIDDEN), F32, kind="ExternalOutput").ap()
    block_program(nc, *args, out)
    result = run_bass_kernel_spmd(nc, [arrays], core_ids=[0])
    return result.results[0]["out"].reshape(shape)
```
